# Optimizing a Trainium2 kernel written in Bass

```python
import numpy as np
import jax
import jax.numpy as jnp

def _softmax(x, axis=-1):
    return jax.nn.softmax(x, axis=axis)

def _gelu(x):
    return jax.nn.gelu(x, approximate=True)

def _silu(x):
    return jax.nn.silu(x)

def _sigmoid(x):
    return jax.nn.sigmoid(x)

def _layernorm(x, axis=-1, eps=1e-05):
    m = jnp.mean(x, axis=axis, keepdims=True)
    v = jnp.var(x, axis=axis, keepdims=True)
    return (x - m) / jnp.sqrt(v + eps)

def _scatter_add(tgt, idx, src, axis=0):
    return tgt.at[idx].add(src)

def _segment_sum(src, seg, n):
    return jax.ops.segment_sum(src, seg, n)
kernel_name = 'mk_macaron_d1_jaxref_r4_72dc9d'

def setup_inputs(seed: int=0):
    np.random.seed(seed)
    _w = jnp.asarray

    def _L0_attn_setup():
        import jax, jax.numpy as jnp
        import numpy as np
        D_MODEL, D_K, D_V, N_HEADS = (256, 64, 64, 16)
        B, T = (4, 512)

        def _xavier(key, shape, gain):
            fan_in, fan_out = (shape[0], shape[1])
            a = gain * np.sqrt(6.0 / (fan_in + fan_out))
            return jax.random.uniform(key, shape, jnp.float32, -a, a)
        key = jax.random.key(seed)
        ks = jax.random.split(key, 6)
        H, dk, dv, d = (N_HEADS, D_K, D_V, D_MODEL)
        return {'x': jax.random.normal(ks[0], (B, T, d), jnp.float32), 'W_q': _xavier(ks[1], (d, H * dk), 0.1), 'W_k': _xavier(ks[2], (d, H * dk), 0.1), 'W_v': _xavier(ks[3], (d, H * dv), 0.1), 'W_gate': _xavier(ks[4], (d, H * dk), 0.01), 'b_gate': jnp.full((H * dk,), 3.0, jnp.float32), 'W_o': _xavier(ks[5], (H * dv, d), 0.1)}
    _L0_attn_in = _L0_attn_setup()

    def _L0_ffn_setup():
        import jax, jax.numpy as jnp
        import numpy as np
        B, T, C = (8, 512, 256)
        H = 1024
        E = 8
        K = 2
        LOAD_FACTOR = 1.2
        N_LAYER = 12

        def _get_expert_inputs(x, logits, expert_capacity):
            Tt = logits.shape[0]
            Cc = x.shape[1]
            top_k_logits, expert_indices = jax.lax.top_k(logits, K)
            expert_probs = jax.nn.softmax(top_k_logits, axis=-1)
            ei = jnp.swapaxes(expert_indices, 0, 1).ravel()
            one_hot = jax.nn.one_hot(ei, E, dtype=jnp.int32)
            pos = jnp.cumsum(one_hot, axis=0) * one_hot - 1
            pos = pos.reshape(-1, Tt, E)
            pos = jnp.swapaxes(pos, 0, 1)
            pos = jnp.max(pos, axis=2)
            ei = jnp.swapaxes(ei.reshape(-1, Tt), 0, 1)
            buf = jnp.zeros((E, expert_capacity, Cc), x.dtype)
            xr = jnp.repeat(x, K, axis=0)
            expert_inputs = buf.at[ei.ravel(), pos.ravel()].add(xr)
            return (expert_probs, pos, ei, expert_inputs)
        key = jax.random.key(seed)
        ks = jax.random.split(key, 9)
        std = 0.02
        proj_std = 0.02 * (2 * N_LAYER) ** (-0.5)
        return {'x': jax.random.normal(ks[0], (B, T, C), jnp.float32), 'router_w': jax.random.normal(ks[1], (C, E), jnp.float32) * std, 'router_b': jnp.zeros((E,), jnp.float32), 'w_c_fc': jax.random.normal(ks[2], (E, C, H), jnp.float32) * std, 'b_c_fc': jnp.zeros((E, 1, H), jnp.float32), 'w_gate': jax.random.normal(ks[3], (E, C, H), jnp.float32) * std, 'b_gate': jnp.zeros((E, 1, H), jnp.float32), 'w_c_proj': jax.random.normal(ks[4], (E, H, C), jnp.float32) * proj_std, 'b_c_proj': jnp.zeros((E, 1, C), jnp.float32)}
    _L0_ffn_in = _L0_ffn_setup()
    _d = {'L0_attn_x': _L0_attn_in['x'], 'L0_attn_W_q': _L0_attn_in['W_q'], 'L0_attn_W_k': _L0_attn_in['W_k'], 'L0_attn_W_v': _L0_attn_in['W_v'], 'L0_attn_W_gate': _L0_attn_in['W_gate'], 'L0_attn_b_gate': _L0_attn_in['b_gate'], 'L0_attn_W_o': _L0_attn_in['W_o'], 'L0_ffn_router_w': _L0_ffn_in['router_w'], 'L0_ffn_router_b': _L0_ffn_in['router_b'], 'L0_ffn_w_c_fc': _L0_ffn_in['w_c_fc'], 'L0_ffn_b_c_fc': _L0_ffn_in['b_c_fc'], 'L0_ffn_w_gate': _L0_ffn_in['w_gate'], 'L0_ffn_b_gate': _L0_ffn_in['b_gate'], 'L0_ffn_w_c_proj': _L0_ffn_in['w_c_proj'], 'L0_ffn_b_c_proj': _L0_ffn_in['b_c_proj']}
    _x0 = _d['L0_attn_x']
    _d['L0_attn_x'] = jax.random.normal(jax.random.fold_in(jax.random.key(seed), 1), (1, 4096, 256), dtype=_x0.dtype)
    del _x0
    return _d

def reference(L0_attn_x, L0_attn_W_q, L0_attn_W_k, L0_attn_W_v, L0_attn_W_gate, L0_attn_b_gate, L0_attn_W_o, L0_ffn_router_w, L0_ffn_router_b, L0_ffn_w_c_fc, L0_ffn_b_c_fc, L0_ffn_w_gate, L0_ffn_b_gate, L0_ffn_w_c_proj, L0_ffn_b_c_proj):

    def _L0_attn_ref(x, W_q, W_k, W_v, W_gate, b_gate, W_o):
        import jax, jax.numpy as jnp
        import numpy as np
        D_MODEL, D_K, D_V, N_HEADS = (256, 64, 64, 16)
        B, T = (4, 512)

        def _xavier(key, shape, gain):
            fan_in, fan_out = (shape[0], shape[1])
            a = gain * np.sqrt(6.0 / (fan_in + fan_out))
            return jax.random.uniform(key, shape, jnp.float32, -a, a)
        Bn, Tn, d = x.shape
        H, dk, dv = (N_HEADS, D_K, D_V)
        q = (x @ W_q).reshape(Bn, Tn, H, dk)
        k = (x @ W_k).reshape(Bn, Tn, H, dk)
        v = (x @ W_v).reshape(Bn, Tn, H, dv)
        a = jax.nn.sigmoid(x @ W_gate + b_gate).reshape(Bn, Tn, H, dk)

        def step(S, qkva):
            q_t, k_t, v_t, a_t = qkva
            S = a_t[..., None] * S + k_t[..., None] * v_t[..., None, :]
            o_t = jnp.einsum('bhk,bhkv->bhv', q_t, S)
            return (S, o_t)
        S0 = jnp.zeros((Bn, H, dk, dv), x.dtype)
        qs = jnp.moveaxis(q, 1, 0)
        ks_ = jnp.moveaxis(k, 1, 0)
        vs = jnp.moveaxis(v, 1, 0)
        as_ = jnp.moveaxis(a, 1, 0)
        _, outs = jax.lax.scan(step, S0, (qs, ks_, vs, as_))
        out = jnp.moveaxis(outs, 0, 1).reshape(Bn, Tn, H * dv)
        return out @ W_o

    def _L0_ffn_ref(x, router_w, router_b, w_c_fc, b_c_fc, w_gate, b_gate, w_c_proj, b_c_proj):
        import jax, jax.numpy as jnp
        import numpy as np
        B, T, C = (8, 512, 256)
        H = 1024
        E = 8
        K = 2
        LOAD_FACTOR = 1.2
        N_LAYER = 12

        def _get_expert_inputs(x, logits, expert_capacity):
            Tt = logits.shape[0]
            Cc = x.shape[1]
            top_k_logits, expert_indices = jax.lax.top_k(logits, K)
            expert_probs = jax.nn.softmax(top_k_logits, axis=-1)
            ei = jnp.swapaxes(expert_indices, 0, 1).ravel()
            one_hot = jax.nn.one_hot(ei, E, dtype=jnp.int32)
            pos = jnp.cumsum(one_hot, axis=0) * one_hot - 1
            pos = pos.reshape(-1, Tt, E)
            pos = jnp.swapaxes(pos, 0, 1)
            pos = jnp.max(pos, axis=2)
            ei = jnp.swapaxes(ei.reshape(-1, Tt), 0, 1)
            buf = jnp.zeros((E, expert_capacity, Cc), x.dtype)
            xr = jnp.repeat(x, K, axis=0)
            expert_inputs = buf.at[ei.ravel(), pos.ravel()].add(xr)
            return (expert_probs, pos, ei, expert_inputs)
        Bb, Tt, Cc = x.shape
        logits = jnp.einsum('btc,ce->bte', x, router_w) + router_b
        cap = int(LOAD_FACTOR * K * Tt // E)
        probs, pos, idx, einp = jax.vmap(lambda xb, lb: _get_expert_inputs(xb, lb, cap))(x, logits)
        if Bb % E == 0:
            t = einp.reshape(E, Bb // E, E, cap, Cc)
            t = jnp.swapaxes(t, 0, 2)
        else:
            t = jnp.swapaxes(einp, 0, 1)
        einp2 = t.reshape(E, Bb * cap, Cc)
        h = jnp.einsum('eti,eih->eth', einp2, w_c_fc) + b_c_fc
        g = jnp.einsum('eti,eih->eth', einp2, w_gate) + b_gate
        o = jnp.einsum('eth,eho->eto', jax.nn.silu(h * g), w_c_proj) + b_c_proj
        if Bb % E == 0:
            o = o.reshape(E, Bb // E, E, cap, Cc)
            o = jnp.swapaxes(o, 0, 2)
            o = o.reshape(Bb, E, cap, Cc)
        else:
            o = o.reshape(E, Bb, cap, Cc)
            o = jnp.swapaxes(o, 0, 1)

        def collect(eo, i, p, pr):
            sel = eo[i, p]
            return jnp.sum(pr[..., None] * sel, axis=1)
        return jax.vmap(collect)(o, idx, pos, probs)
    x = L0_attn_x
    x = x + 0.5 * _L0_ffn_ref(_layernorm(x, axis=-1), L0_ffn_router_w, L0_ffn_router_b, L0_ffn_w_c_fc, L0_ffn_b_c_fc, L0_ffn_w_gate, L0_ffn_b_gate, L0_ffn_w_c_proj, L0_ffn_b_c_proj)
    x = x + _L0_attn_ref(_layernorm(x, axis=-1), L0_attn_W_q, L0_attn_W_k, L0_attn_W_v, L0_attn_W_gate, L0_attn_b_gate, L0_attn_W_o)
    x = x + 0.5 * _L0_ffn_ref(_layernorm(x, axis=-1), L0_ffn_router_w, L0_ffn_router_b, L0_ffn_w_c_fc, L0_ffn_b_c_fc, L0_ffn_w_gate, L0_ffn_b_gate, L0_ffn_w_c_proj, L0_ffn_b_c_proj)
    return x

_drawn_inputs = setup_inputs


def setup_inputs(seed=0):
    import zlib

    import numpy as np

    out = dict(_drawn_inputs(seed))
    spreads = {'L0_attn_b_gate': (3.0, 0.6),
     'L0_ffn_router_b': (0.0, 0.1),
     'L0_ffn_b_c_fc': (0.0, 0.8),
     'L0_ffn_b_gate': (0.0, 0.8),
     'L0_ffn_b_c_proj': (0.0, 0.1)}
    factors = {'L0_attn_W_q': 8.0,
     'L0_attn_W_k': 8.0,
     'L0_attn_W_v': 8.0,
     'L0_attn_W_gate': 64.0,
     'L0_attn_W_o': 8.0,
     'L0_ffn_w_c_fc': 8.0,
     'L0_ffn_w_gate': 8.0,
     'L0_ffn_w_c_proj': 8.0}
    for name, (base, spread) in spreads.items():
        noise = np.random.default_rng([zlib.crc32(name.encode()), seed]).standard_normal(out[name].shape)
        drawn = base * np.exp(spread * noise) if base else spread * noise
        out[name] = jnp.asarray(drawn.astype(out[name].dtype))
    for name, factor in factors.items():
        out[name] = (out[name] * factor).astype(out[name].dtype)
    return out
```

```python
from contextlib import ExitStack

import concourse.bass as bass
from concourse import mybir

ALU = mybir.AluOpType
ACT = mybir.ActivationFunctionType
AX_X = mybir.AxisListType.X
F32 = mybir.dt.float32
F32R = mybir.dt.float32r
BF16 = mybir.dt.bfloat16
U32 = mybir.dt.uint32

P = 128
T = 4096
C = 256
KC = C // P
TILES = T // P
EPS = 1e-5

E = 8
TOPK = 2
HID = 1024
HJ = HID // P
CAP = int(1.2 * TOPK * T // E)
ROWS = E * CAP
PICKS = TOPK * TILES
SKIP = 1 << 17
BIG = 1e30
GROUPS = [(s, min(512, CAP - s)) for s in range(0, CAP, 512)]
GROUP_TILES = [[(o, min(P, n - o)) for o in range(0, n, P)] for _, n in GROUPS]
Y_TILES = sum(len(t) for t in GROUP_TILES)
NG = len(GROUPS)
UNITS = NG * HJ

HEADS = 16
DH = 64
NPAIR = HEADS * DH // P
SUPER = 4
NSUP = TILES // SUPER
SW = SUPER * P
HALF = P // 2
TINY = 1e-30

CLEAR_ROWS = 8
CLEAR = CLEAR_ROWS * P
CLEARS = -(-ROWS // CLEAR)
CONSTS = 7
ATT_CLEARS = 4
RING = 16
assert ROWS % CLEAR_ROWS == 0 and NG == 3 and Y_TILES % 2 == 0


class Steps:

    def __init__(self, eng, sem):
        self.eng, self.sem, self.base, self.n = eng, sem, 0, 0

    def after(self, ins):
        ins.then_inc(self.sem, 1)
        self.n += 1
        self.eng.wait_ge(self.sem, self.base + self.n)

    def loop(self, lo, hi, per, body):
        start = self.base + self.n
        with self.eng.Fori(lo, hi) as i:
            self.base, self.n = start + (i - lo) * per, 0
            body(i)
            assert self.n == per, (self.n, per)
        self.base, self.n = start + (hi - lo) * per, 0


def macaron(nc, x_in, w_q, w_k, w_v, w_gate, b_gate, w_o, router_w, router_b,
            w_fc, b_fc, w_g, b_g, w_proj, b_proj, out):
    with ExitStack() as ctx:
        def sb(name, shape, dt=F32):
            return ctx.enter_context(nc.sbuf_tensor(name, shape, dt))

        def sem(name):
            return ctx.enter_context(nc.semaphore(name))

        expert_in = nc.dram_tensor("expert_in", (ROWS, C), F32, kind="Internal").ap()
        expert_out = nc.dram_tensor("expert_out", (ROWS, C), F32, kind="Internal").ap()

        x = sb("x", [P, TILES, C])
        wide = sb("wide", [P, 8192])
        temp = sb("temp", [P, 2048])
        rows = sb("rows", [P, 1024])
        halves = sb("halves", [P, 32768], F32R)
        ident = sb("ident", [P, P])
        causal = sb("causal", [P, P], BF16)
        before = sb("before", [P, P], BF16)
        head_of = sb("head_of", [P, 2])
        zeros = sb("zeros", [P, HALF], BF16)
        rank = sb("rank", [P, E])
        router = sb("router", [P, KC, E])
        router_bias = sb("router_bias", [P, E])
        rstd = sb("rstd", [P, TILES])
        read_slot = sb("read_slot", [P, PICKS], U32)
        weight1 = sb("weight1", [P, TILES])
        weight2 = sb("weight2", [P, TILES])
        bias_fc = sb("bias_fc", [P, E * HJ])
        bias_g = sb("bias_g", [P, E * HJ])
        bias_gate = sb("bias_gate", [P, NPAIR])
        stats = sb("stats", [P, TILES, 6])
        bias_now = sb("bias_now", [P, HJ])
        enter = sb("enter", [P, SUPER])
        carry = sb("carry", [P, SUPER])
        state_sum = sb("state_sum", [P, P])

        def part(t, at, *dims):
            n = 1
            for d in dims:
                n *= d
            v = t[:, at:at + n]
            names = "abc"[:len(dims)]
            if len(dims) == 1:
                return v
            return v.rearrange(f"p ({' '.join(names)}) -> p {' '.join(names)}",
                               **{names[i]: dims[i] for i in range(1, len(dims))})

        xn = part(wide, 0, TILES, C)
        raw_fc = part(wide, 0, KC, HID)
        raw_g = part(wide, 2048, KC, HID)
        raw_proj = part(wide, 4096, HJ, C)
        xg = [part(wide, 6144, 4, C), part(wide, 7168, 4, C)]
        got = part(wide, 0, RING, TOPK, C)
        g_sb = [part(temp, 0, 512), part(temp, 512, 512)]
        hg = [part(temp, 1024, 512), part(temp, 1536, 512)]
        y_sb = part(rows, 0, 2, C)
        xn_tile = part(rows, 0, 2, C)
        y_bias = part(rows, 512, C)
        fc_hi, fc_lo, gw_hi, gw_lo = (part(halves, 2048 * i, KC, HID) for i in range(4))
        pr_hi, pr_lo = (part(halves, 2048 * i, HJ, C) for i in (4, 5))
        s_hi = [part(halves, 12288 + 8192 * i, HJ, 512) for i in range(2)]
        s_lo = [part(halves, 16384 + 8192 * i, HJ, 512) for i in range(2)]
        xt_hi = [part(halves, 28672 + 2048 * i, KC, 512) for i in range(2)]
        xt_lo = [part(halves, 29696 + 2048 * i, KC, 512) for i in range(2)]
        xnt = [part(temp, 0, KC, P), part(temp, 256, KC, P)]
        logits = part(temp, 512, TILES, E)
        eq = part(temp, 768, TILES, E)
        taken = part(temp, 1024, 512)
        small = part(temp, 1536, 128)
        hot = part(temp, 1664, 256).bitcast(BF16)
        resume = part(temp, 0, 256).bitcast(BF16)
        top1, top2 = small[:, 0:32], small[:, 32:64]
        rank12 = small[:, 64:128]
        pos = part(temp, 256, PICKS)
        slot = part(temp, 320, PICKS)
        over = part(temp, 384, PICKS)
        ones = part(temp, 1984, P // 2).bitcast(BF16)
        write_slot = part(temp, 1920, PICKS).bitcast(U32)
        v_sb = part(wide, 0, SUPER, HEADS * DH)
        decay = part(wide, 4096, SUPER, P)
        near = part(wide, 4608, SUPER, P)
        far = part(wide, 5120, SUPER, P)
        qd = [part(wide, 5632, SUPER, P), part(wide, 6144, SUPER, P)]
        kd = part(wide, 6656, SUPER, P)
        prob = [part(wide, 7168, SUPER, P), part(wide, 7680, SUPER, P)]
        kdt = part(temp, 0, SUPER, P)
        state_in = part(temp, 512, SUPER, P)
        state = part(temp, 1024, NPAIR, P)
        xna = part(rows, 0, SUPER, C)
        raw_w = part(temp, 0, 2048)
        wq, wk, wz, wv = ([part(halves, 4096 * i, KC, 1024), part(halves, 4096 * i + 2048, KC, 1024)]
                          for i in range(4))
        wo = [part(halves, 16384, NPAIR, C), part(halves, 18432, NPAIR, C)]
        xa = [part(halves, 20480, KC, SW), part(halves, 21504, KC, SW)]
        ot = [part(halves, 22528, NPAIR, SW), part(halves, 26624, NPAIR, SW)]

        bank = [ctx.enter_context(nc.psum_tensor(f"bank{i}", [P, 512], F32)) for i in range(8)]

        x_loaded = [sem(f"x_loaded{i}") for i in range(4)]
        small_loaded = sem("small_loaded")
        consts_made = sem("consts_made")
        pool_steps = sem("pool_steps")
        zero_made = sem("zero_made")
        cleared = sem("cleared")
        bias_turned, bias_set = sem("bias_turned"), sem("bias_set")
        stats_made, x_settled = sem("stats_made"), sem("x_settled")
        dve_steps = sem("dve_steps")
        act_steps = sem("act_steps")
        var_made = sem("var_made")
        std_made = sem("std_made")
        xn_made, xn_kept = sem("xn_made"), sem("xn_kept")
        xn_turned = sem("xn_turned")
        xnt_copied = sem("xnt_copied")
        logits_done = sem("logits_done")
        gap_made = sem("gap_made")
        exp_made = sem("exp_made")
        hot_made = sem("hot_made")
        counted = sem("counted")
        slots_made = sem("slots_made")
        scattered = sem("scattered")
        fc_staged = sem("fc_staged")
        proj_staged = sem("proj_staged")
        fc_hi_made, fc_split = sem("fc_hi_made"), sem("fc_split")
        proj_hi_made, proj_split = sem("proj_hi_made"), sem("proj_split")
        bias_loaded = sem("bias_loaded")
        xg_loaded = [sem("xg_loaded0"), sem("xg_loaded1")]
        xg_turned = sem("xg_turned")
        xt_hi_made, xt_split = sem("xt_hi_made"), sem("xt_split")
        up_done = sem("up_done")
        g_copied = sem("g_copied")
        hg_made = sem("hg_made")
        silu_made = sem("silu_made")
        s_hi_made, s_split = sem("s_hi_made"), sem("s_split")
        y_done = sem("y_done")
        y_copied = sem("y_copied")
        y_stored = [sem("y_stored0"), sem("y_stored1")]
        rows_got = [sem(f"rows_got{i}") for i in range(RING)]
        row1_added, combined = sem("row1_added"), sem("combined")
        aw_staged, aw_hi_made, aw_split = sem("aw_staged"), sem("aw_hi_made"), sem("aw_split")
        att_cleared = sem("att_cleared")
        xna_made, xna_turned = sem("xna_made"), sem("xna_turned")
        xa_hi_made, xa_split = sem("xa_hi_made"), sem("xa_split")
        z_done, qk_done = sem("z_done"), sem("qk_done")
        decay_made, qk_made = sem("decay_made"), sem("qk_made")
        v_done, v_copied = sem("v_done"), sem("v_copied")
        k_turned, kdt_copied = sem("k_turned"), sem("kdt_copied")
        scores_done, prob_made = sem("scores_done"), sem("prob_made")
        kv_done, state_ready, state_kept = sem("kv_done"), sem("state_ready"), sem("state_kept")
        o_done, ot_hi_made, ot_split = sem("o_done"), sem("ot_hi_made"), sem("ot_split")
        wo_done, wo_added = sem("wo_done"), sem("wo_added")
        stored = sem("stored")

        block = ctx.enter_context(nc.Block())

        def as_f32(ap):
            return ap.bitcast(F32)

        def passes(hi_lo_a, hi_lo_b):
            (ah, al), (bh, bl) = hi_lo_a, hi_lo_b
            return [(ah, bh), (ah, bl), (al, bh)]

        tok = "(i p) c -> p i c"

        @block.sync
        def _(sp):
            for i in range(4):
                n = TILES // 4
                sp.dma_start(x[:, i * n:(i + 1) * n, :],
                             x_in[0, i * n * P:(i + 1) * n * P, :].rearrange(tok, p=P)).then_inc(x_loaded[i], 16)
            sp.wait_ge(zero_made, 1)
            for at in range(0, ROWS, CLEAR):
                n = min(CLEAR, ROWS - at) // CLEAR_ROWS
                sp.dma_start(expert_in[at:at + n * CLEAR_ROWS, :].rearrange("(p a) c -> p (a c)", a=CLEAR_ROWS),
                             as_f32(halves[0:n, 0:CLEAR_ROWS * C])).then_inc(cleared, 16)

            def load_rows(r, e, n):
                u = r * E + e
                sp.wait_ge(xg_turned, [u * NG, u * NG, u * NG + 1][n])
                buf = n % 2
                s, m = GROUPS[n]
                full = m // P
                at = e * CAP + s
                sp.dma_start(xg[buf][:, 0:full, :],
                             expert_in[bass.ds(at, full * P), :].rearrange(tok, p=P)).then_inc(xg_loaded[buf], 16)
                if m % P:
                    sp.dma_start(xg[buf][0:m % P, full, :],
                                 expert_in[bass.ds(at + full * P, m % P), :]).then_inc(xg_loaded[buf], 16)

            def stage_fc(r, e):
                sp.wait_ge(fc_split, (r * E + e) * 8)
                sp.dma_start(raw_fc, w_fc[e].rearrange("(a p) n -> p a n", p=P)).then_inc(fc_staged, 16)
                sp.dma_start(raw_g, w_g[e].rearrange("(a p) n -> p a n", p=P)).then_inc(fc_staged, 16)

            def stage_proj(r, e):
                sp.wait_ge(proj_split, (r * E + e) * 4)
                sp.dma_start(raw_proj, w_proj[e].rearrange("(a p) n -> p a n", p=P)).then_inc(proj_staged, 16)

            def load_bias(r, e):
                sp.dma_start(y_bias, b_proj[e].to_broadcast([P, C])).then_inc(bias_loaded, 16)

            def store_y(r, e, t):
                u = r * E + e
                sp.wait_ge(y_copied, u * Y_TILES + t + 1)
                n = t // 4 if t < 8 else 2
                o, m = GROUP_TILES[n][t - 4 * n]
                at = e * CAP + GROUPS[n][0] + o
                sp.dma_start(expert_out[bass.ds(at, m), :], y_sb[0:m, t % 2, :]).then_inc(y_stored[t % 2], 16)

            def expert(r, e, last):
                load_rows(r, e, 2)
                if not last:
                    stage_fc(r, e + 1)
                    stage_proj(r, e + 1)
                for t in range(4):
                    store_y(r, e, t)
                if not last:
                    load_rows(r, e + 1, 0)
                    load_rows(r, e + 1, 1)
                for t in range(4, Y_TILES):
                    store_y(r, e, t)
                if not last:
                    load_bias(r, e + 1)

            for r in range(2):
                sp.wait_ge(scattered, (r + 1) * PICKS * 16)
                load_rows(r, 0, 0)
                stage_fc(r, 0)
                load_rows(r, 0, 1)
                stage_proj(r, 0)
                load_bias(r, 0)
                with sp.Fori(0, E - 1) as e:
                    expert(r, e, False)
                expert(r, E - 1, True)
                if r == 0:
                    for n, w in enumerate((w_q, w_k, w_gate, w_v, w_o)):
                        if n:
                            sp.wait_ge(aw_split, n)
                        sp.dma_start(raw_w.rearrange("p (a n) -> p a n", a=w.shape[0] // P),
                                     w.rearrange("(a p) n -> p a n", p=P)).then_inc(aw_staged, 16)
            with sp.Fori(0, TILES) as i:
                sp.wait_ge(combined, TILES + i + 1)
                sp.dma_start(out[0, bass.ds(i * P, P), :], x[:, bass.ds(i, 1), :].rearrange("p a c -> p (a c)")).then_inc(stored, 16)
            sp.wait_ge(stored, TILES * 16)

        @block.gpsimd
        def _(pool):
            steps = Steps(pool, pool_steps)
            steps.after(nc.gpsimd.memset(ident[:], 0.0))
            steps.after(nc.gpsimd.memset(causal[:], 1.0))
            steps.after(nc.gpsimd.memset(before[:], 1.0))
            steps.after(nc.gpsimd.memset(head_of[:], 1.0))
            nc.gpsimd.affine_select(out=ident[:], in_=ident[:], compare_op=ALU.not_equal, fill=1.0, base=0,
                                    pattern=[[-1, P]], channel_multiplier=1).then_inc(consts_made, 1)
            nc.gpsimd.affine_select(out=causal[:], in_=causal[:], compare_op=ALU.is_ge, fill=0.0, base=0,
                                    pattern=[[1, P]], channel_multiplier=-1).then_inc(consts_made, 1)
            nc.gpsimd.affine_select(out=before[:], in_=before[:], compare_op=ALU.is_gt, fill=0.0, base=0,
                                    pattern=[[1, P]], channel_multiplier=-1).then_inc(consts_made, 1)
            nc.gpsimd.affine_select(out=head_of[:, 0:1], in_=head_of[:, 0:1], compare_op=ALU.is_ge, fill=0.0,
                                    base=DH - 1, pattern=[[0, 1]], channel_multiplier=-1).then_inc(consts_made, 1)
            nc.gpsimd.affine_select(out=head_of[:, 1:2], in_=head_of[:, 1:2], compare_op=ALU.is_ge, fill=0.0,
                                    base=-DH, pattern=[[0, 1]], channel_multiplier=1).then_inc(consts_made, 1)
            nc.gpsimd.memset(zeros[:], 0.0).then_inc(consts_made, 1)
            nc.gpsimd.iota(rank[:], [[-1, E]], base=E, channel_multiplier=0,
                           allow_small_or_imprecise_dtypes=True).then_inc(consts_made, 1)
            pool.dma_start(router[:], router_w.rearrange("(a p) e -> p a e", p=P)).then_inc(small_loaded, 16)
            pool.dma_start(router_bias[:], router_b.rearrange("(a e) -> a e", a=1).to_broadcast([P, E])).then_inc(small_loaded, 16)
            pool.dma_start(rows[0:E * HJ, 0:P], b_fc.rearrange("e a (j p) -> (e a j) p", p=P)).then_inc(small_loaded, 16)
            pool.dma_start(rows[0:E * HJ, P:2 * P], b_g.rearrange("e a (j p) -> (e a j) p", p=P)).then_inc(small_loaded, 16)
            pool.dma_start(rows[0:NPAIR, 2 * P:3 * P], b_gate.rearrange("(j p) -> j p", p=P)).then_inc(small_loaded, 16)
            for r in range(2):
                pool.wait_ge(slots_made, r + 1)
                if r == 0:
                    pool.wait_ge(cleared, CLEARS * 16)
                for k in range(PICKS):
                    pool.indirect_dma_start(expert_in, bass.IndirectOffsetOnAxis(ap=write_slot[:, k:k + 1], axis=0),
                                            xn[:, k % TILES, :], None, bounds_check=ROWS - 1,
                                            oob_is_err=False).then_inc(scattered, 16)
                for b in range(2):
                    pool.wait_ge(y_stored[b], (r + 1) * E * Y_TILES // 2 * 16)
                for i in range(TILES):
                    if i >= RING:
                        pool.wait_ge(combined, r * TILES + i - RING + 1)
                    for k in range(TOPK):
                        j = k * TILES + i
                        pool.indirect_dma_start(got[:, i % RING, k, :], None, expert_out,
                                                bass.IndirectOffsetOnAxis(ap=read_slot[:, j:j + 1], axis=0)
                                                ).then_inc(rows_got[i % RING], 16)

        @block.tensor
        def _(pe):
            pe.wait_ge(consts_made, CONSTS)
            pe.wait_ge(small_loaded, 16 * 5)
            for n, (k, at) in enumerate(((E * HJ, 0), (E * HJ, P), (NPAIR, 2 * P))):
                pe.transpose(bank[n][:, 0:k], rows[0:k, at:at + P], ident[0:k, 0:k]).then_inc(bias_turned, 1)

            def route(r):
                with pe.Fori(0, TILES // 2) as j:
                    for b in range(2):
                        pe.wait_ge(xn_made, r * TILES + j * 2 + b + 1)
                        for kc in range(KC):
                            m = pe.transpose(bank[b][:, kc * P:(kc + 1) * P],
                                             xn_tile[:, b, kc * P:(kc + 1) * P], ident[:])
                        m.then_inc(xn_turned, 1)
                    for b in range(2):
                        pe.wait_ge(xnt_copied, r * TILES + j * 2 + b + 1)
                        for kc in range(KC):
                            m = pe.matmul(bank[2][:, bass.ds((j * 2 + b) * E, E)], xnt[b][:, kc, :], router[:, kc, :],
                                          start=(kc == 0), stop=(kc == KC - 1))
                        m.then_inc(logits_done, 1)
                pe.wait_ge(hot_made, r + 1)
                pe.matmul(bank[3][:], before[:], hot, start=True, stop=True)
                pe.matmul(bank[4][:], ones, hot, start=True, stop=True).then_inc(counted, 1)

            def turn(r, e, n):
                u = r * E + e
                buf = n % 2
                pe.wait_ge(xg_loaded[buf], [u * 48 + 16, u * 16 + 16, u * 48 + 48][n])
                pe.wait_ge(xt_split, u * NG + n)
                for kc in range(KC):
                    for i, (o, m) in enumerate(GROUP_TILES[n]):
                        t = pe.transpose(bank[6 + kc][:, o:o + m], xg[buf][0:m, i, kc * P:(kc + 1) * P],
                                         ident[0:m, 0:m])
                t.then_inc(xg_turned, 1)

            def up(r, e, n, js):
                u = r * E + e
                buf, w = n % 2, GROUPS[n][1]
                if js[0] == 0:
                    pe.wait_ge(xt_split, u * NG + n + 1)
                    if n == 0:
                        pe.wait_ge(fc_split, u * 8 + 8)
                for j in js:
                    unit = n * HJ + j
                    b = unit % 2
                    if unit >= 2:
                        pe.wait_ge(hg_made, u * UNITS + unit - 1)
                    for at, hi_lo in ((0, (fc_hi, fc_lo)), (2, (gw_hi, gw_lo))):
                        ps = [(kc, a, v) for kc in range(KC) for a, v in passes(hi_lo, (xt_hi[buf], xt_lo[buf]))]
                        for i, (kc, a, v) in enumerate(ps):
                            m = pe.matmul(bank[at + b][:, 0:w], a[:, kc, j * P:(j + 1) * P], v[:, kc, 0:w],
                                          start=(i == 0), stop=(i == len(ps) - 1))
                    m.then_inc(up_done, 1)

            def down(r, e, n):
                u = r * E + e
                buf = n % 2
                pe.wait_ge(s_split, u * UNITS + (n + 1) * HJ)
                if n == 0:
                    pe.wait_ge(proj_split, u * 4 + 4)
                for i, (o, m) in enumerate(GROUP_TILES[n]):
                    t = 4 * n + i
                    if t >= 2:
                        pe.wait_ge(y_copied, u * Y_TILES + t - 1)
                    ps = [(j, a, v) for j in range(HJ)
                          for a, v in passes((s_hi[buf], s_lo[buf]), (pr_hi, pr_lo))]
                    for k, (j, a, v) in enumerate(ps):
                        mm = pe.matmul(bank[4 + t % 2][0:m, 0:C], a[:, j, o:o + m], v[:, j, :],
                                       start=(k == 0), stop=(k == len(ps) - 1))
                    mm.then_inc(y_done, 1)

            def expert(r, e):
                first, second = range(HJ // 2), range(HJ // 2, HJ)
                turn(r, e, 0)
                up(r, e, 0, first)
                turn(r, e, 1)
                up(r, e, 0, second)
                up(r, e, 1, first)
                turn(r, e, 2)
                up(r, e, 1, second)
                down(r, e, 0)
                up(r, e, 2, range(HJ))
                down(r, e, 1)
                down(r, e, 2)

            def attention():
                pe.wait_ge(aw_split, 5)
                pe.wait_ge(att_cleared, ATT_CLEARS)
                with pe.Fori(0, NSUP) as s:
                    pe.wait_ge(wo_added, s * SUPER)
                    pe.wait_ge(xna_made, s * SUPER + SUPER)
                    for kc in range(KC):
                        for b in range(SUPER):
                            m = pe.transpose(bank[3 + kc][:, b * P:(b + 1) * P], xna[:, b, kc * P:(kc + 1) * P], ident[:])
                    m.then_inc(xna_turned, 1)
                    pe.wait_ge(xa_split, s * KC + KC)

                    def project(g):
                        for at, w, done in ((2, wz, z_done), (0, wq, None), (1, wk, qk_done)):
                            ps = [(kc, a, v) for kc in range(KC) for a, v in passes(w, xa)]
                            for i, (kc, a, v) in enumerate(ps):
                                m = pe.matmul(bank[at][:], a[:, kc, g * P:(g + 1) * P], v[:, kc, :],
                                              start=(i == 0), stop=(i == len(ps) - 1))
                            if done is not None:
                                m.then_inc(done, 1)

                    def inside(g):
                        G = s * NPAIR + g
                        pe.wait_ge(qk_made, G + 1)
                        for c in range(SUPER):
                            m = pe.transpose(bank[6][:, c * P:(c + 1) * P], kd[:, c, :], ident[:])
                        m.then_inc(k_turned, 1)
                        for c in range(SUPER):
                            for h in range(2):
                                hp = slice(h * DH, (h + 1) * DH)
                                m = pe.matmul(bank[3 + h][:, c * P:(c + 1) * P], kd[hp, c, :], qd[g % 2][hp, c, :],
                                              start=True, stop=True)
                        m.then_inc(scores_done, 1)
                        pe.wait_ge(kdt_copied, G + 1)
                        pe.wait_ge(state_kept, G)
                        for c in range(SUPER):
                            m = pe.matmul(bank[7][:, c * P:(c + 1) * P], kdt[:, c, :], v_sb[:, c, g * P:(g + 1) * P],
                                          start=True, stop=True)
                        m.then_inc(kv_done, 1)

                    def outputs(g):
                        G = s * NPAIR + g
                        pe.wait_ge(prob_made, G + 1)
                        pe.wait_ge(ot_split, G)
                        for c in range(SUPER):
                            pe.wait_ge(state_ready, G * SUPER + c + 1)
                            cols = slice(c * P, (c + 1) * P)
                            pe.matmul(bank[5][:, cols], state_in[:, c, :], qd[g % 2][:, c, :],
                                      start=True, stop=False, skip_group_check=True)
                            for h in range(2):
                                m = pe.matmul(bank[5][h * DH:(h + 1) * DH, cols],
                                              v_sb[:, c, g * P + h * DH:g * P + (h + 1) * DH], prob[h][:, c, :],
                                              start=False, stop=True, skip_group_check=True)
                        m.then_inc(o_done, 1)

                    project(0)
                    pe.wait_ge(ot_split, s * NPAIR)
                    for b in range(SUPER):
                        for half in range(2):
                            n = 2 * b + half
                            if n >= 2:
                                pe.wait_ge(v_copied, s * 8 + n - 1)
                            ps = [(kc, a, v) for kc in range(KC) for a, v in passes(xa, wv)]
                            for i, (kc, a, v) in enumerate(ps):
                                m = pe.matmul(bank[5 + n % 2][:], a[:, kc, b * P:(b + 1) * P],
                                              v[:, kc, half * 512:(half + 1) * 512],
                                              start=(i == 0), stop=(i == len(ps) - 1))
                            m.then_inc(v_done, 1)
                    pe.wait_ge(v_copied, s * 8 + 8)
                    for g in range(NPAIR):
                        inside(g)
                        if g + 1 < NPAIR:
                            project(g + 1)
                        outputs(g)
                    pe.wait_ge(ot_split, s * NPAIR + NPAIR)
                    for b in range(SUPER):
                        if b >= 2:
                            pe.wait_ge(wo_added, s * SUPER + b - 1)
                        ps = [(g, a, v) for g in range(NPAIR) for a, v in passes(ot, wo)]
                        for i, (g, a, v) in enumerate(ps):
                            m = pe.matmul(bank[3 + b % 2][:, 0:C], a[:, g, b * P:(b + 1) * P], v[:, g, :],
                                          start=(i == 0), stop=(i == len(ps) - 1))
                        m.then_inc(wo_done, 1)

            for r in range(2):
                route(r)
                with pe.Fori(0, E - 1) as e:
                    expert(r, e)
                expert(r, E - 1)
                if r == 0:
                    attention()

        @block.scalar
        def _(act):
            def copy(o, i):
                return nc.scalar.activation(o, i, ACT.Copy)

            steps = Steps(act, act_steps)

            def deviation(n):
                act.wait_ge(var_made, n)
                nc.scalar.activation(rstd[:], rstd[:], ACT.Sqrt).then_inc(std_made, 1)

            def route(r):
                with act.Fori(0, TILES // 2) as j:
                    for b in range(2):
                        act.wait_ge(xn_turned, r * TILES + j * 2 + b + 1)
                        copy(xnt[b].rearrange("p a n -> p (a n)"), bank[b][:, 0:C]).then_inc(xnt_copied, 1)
                act.wait_ge(gap_made, r + 1)
                nc.scalar.activation(weight2[:], weight2[:], ACT.Exp).then_inc(exp_made, 1)

            def split_fc(u, k):
                raw, hi = ((raw_fc, fc_hi), (raw_g, gw_hi))[k // 4]
                at = (slice(None), k % 4 // 2, slice(k % 2 * 512, k % 2 * 512 + 512))
                copy(hi[at], raw[at]).then_inc(fc_hi_made, 1)

            def expert(r, e, last):
                u = r * E + e

                def turned(n):
                    w, buf = GROUPS[n][1], n % 2
                    act.wait_ge(xg_turned, u * NG + n + 1)
                    for kc in range(KC):
                        copy(xt_hi[buf][:, kc, 0:w], bank[6 + kc][:, 0:w]).then_inc(xt_hi_made, 1)

                turned(0)
                for n in range(NG):
                    w, buf = GROUPS[n][1], n % 2
                    for j in range(HJ):
                        if j == HJ // 2 and n + 1 < NG:
                            turned(n + 1)
                        unit = n * HJ + j
                        b = unit % 2
                        if unit == 0:
                            act.wait_ge(bias_set, u + 1)
                        act.wait_ge(up_done, u * UNITS + unit + 1)
                        nc.scalar.activation(g_sb[b][:, 0:w], bank[2 + b][:, 0:w], ACT.Identity,
                                             bias=bias_now[:, j:j + 1]).then_inc(g_copied, 1)
                        act.wait_ge(hg_made, u * UNITS + unit + 1)
                        nc.scalar.activation(hg[b][:, 0:w], hg[b][:, 0:w], ACT.Silu).then_inc(silu_made, 1)
                        act.wait_ge(silu_made, u * UNITS + unit + 1)
                        copy(s_hi[buf][:, j, 0:w], hg[b][:, 0:w]).then_inc(s_hi_made, 1)
                        if 2 <= unit < 6:
                            k = 2 * (unit - 2)
                            act.wait_ge(proj_staged, u * 16 + 16)
                            copy(pr_hi[:, k:k + 2, :], raw_proj[:, k:k + 2, :]).then_inc(proj_hi_made, 1)
                if not last:
                    act.wait_ge(fc_staged, u * 32 + 64)
                    for k in range(8):
                        split_fc(u + 1, k)

            def attention():
                act.wait_ge(y_done, E * Y_TILES)
                for n, w in enumerate((wq, wk, wz, wv, wo)):
                    act.wait_ge(aw_staged, 16 * (n + 1))
                    copy(w[0].rearrange("p a n -> p (a n)"), raw_w).then_inc(aw_hi_made, 1)
                deviation(2)
                with act.Fori(0, NSUP) as s:
                    act.wait_ge(xna_turned, s + 1)
                    for kc in range(KC):
                        copy(xa[0][:, kc, :], bank[3 + kc][:]).then_inc(xa_hi_made, 1)

                    def gate(g):
                        G = s * NPAIR + g
                        act.wait_ge(z_done, G + 1)
                        act.wait_ge(qk_made, G)
                        nc.scalar.activation(decay.rearrange("p a n -> p (a n)"), bank[2][:], ACT.Sigmoid,
                                             bias=bias_gate[:, g:g + 1]).then_inc(decay_made, 1)

                    gate(0)
                    for n in range(2 * SUPER):
                        act.wait_ge(v_done, s * 8 + n + 1)
                        copy(v_sb[:, n // 2, n % 2 * 512:n % 2 * 512 + 512], bank[5 + n % 2][:]).then_inc(v_copied, 1)
                    for g in range(NPAIR):
                        G = s * NPAIR + g
                        act.wait_ge(k_turned, G + 1)
                        copy(kdt.rearrange("p a n -> p (a n)"), bank[6][:]).then_inc(kdt_copied, 1)
                        if g + 1 < NPAIR:
                            gate(g + 1)
                        act.wait_ge(o_done, G + 1)
                        copy(ot[0][:, g, :], bank[5][:]).then_inc(ot_hi_made, 1)

            for r in range(2):
                deviation(2 * r + 1)
                route(r)
                act.wait_ge(fc_staged, r * E * 32 + 32)
                for k in range(8):
                    split_fc(r * E, k)
                with act.Fori(0, E - 1) as e:
                    expert(r, e, False)
                expert(r, E - 1, True)
                if r == 0:
                    attention()

        @block.vector
        def _(dve):
            steps = Steps(dve, dve_steps)
            v = nc.vector

            v.memset(as_f32(halves[:, 0:CLEAR_ROWS * C]), 0.0).then_inc(zero_made, 1)
            dve.wait_ge(small_loaded, 16 * 5)
            dve.wait_ge(consts_made, CONSTS)
            for n, o in enumerate((bias_fc, bias_g, bias_gate)):
                dve.wait_ge(bias_turned, n + 1)
                steps.after(v.tensor_copy(o[:], bank[n][:, 0:o.shape[1]]))

            def tile_of(t, i):
                return t[:, bass.ds(i, 1), :].rearrange("p a c -> p (a c)")

            def tile_stats(i):
                return v.bn_stats(tile_of(stats, i), tile_of(x, i))

            def inverse_deviation(n):
                dve.wait_ge(stats_made, n * TILES)
                mean, var = stats[:, :, 1], stats[:, :, 2]
                steps.after(v.tensor_tensor(rstd[:], stats[:, :, 1], stats[:, :, 4], ALU.subtract))
                steps.after(v.tensor_tensor(rstd[:], rstd[:], rstd[:], ALU.mult))
                steps.after(v.tensor_tensor(var, stats[:, :, 2], stats[:, :, 5], ALU.add))
                steps.after(v.tensor_scalar(var, var, 1.0 / C, None, ALU.mult))
                steps.after(v.scalar_tensor_tensor(var, rstd[:], 0.25, var, ALU.mult, ALU.add))
                steps.after(v.tensor_tensor(mean, stats[:, :, 1], stats[:, :, 4], ALU.add))
                steps.after(v.tensor_scalar(mean, mean, 0.5, None, ALU.mult))
                v.tensor_scalar(rstd[:], var, EPS, None, ALU.add).then_inc(var_made, 1)
                dve.wait_ge(std_made, n)
                steps.after(v.reciprocal(rstd[:], rstd[:]))

            def normalised(o, i):
                return v.tensor_scalar(o, tile_of(x, i), tile_of(stats, i)[:, 1:2], rstd[:, bass.ds(i, 1)],
                                       ALU.subtract, ALU.mult)

            def over_experts(ap):
                return ap.unsqueeze(2).to_broadcast([P, TILES, E])

            def choose(r, scores, top, k):
                steps.after(v.tensor_reduce(top, scores, AX_X, ALU.max))
                steps.after(v.tensor_tensor(eq, scores, over_experts(top), ALU.is_equal))
                steps.after(v.tensor_tensor(eq, eq, rank[:].unsqueeze(1).to_broadcast([P, TILES, E]), ALU.mult))
                best = rank12[:, k * TILES:(k + 1) * TILES]
                steps.after(v.tensor_reduce(best, eq, AX_X, ALU.max))
                steps.after(v.tensor_tensor(eq, rank[:].unsqueeze(1).to_broadcast([P, TILES, E]),
                                            over_experts(best), ALU.is_equal))
                picks = hot.rearrange("p (e j) -> p j e", e=E)[:, k * TILES:(k + 1) * TILES, :]
                return v.tensor_copy(picks, eq)

            def route(r):
                with dve.Fori(0, TILES // 2) as j:
                    dve.wait_ge(xn_turned, r * TILES + j * 2)
                    for b in range(2):
                        normalised(xn_tile[:, b, :], j * 2 + b).then_inc(xn_made, 1)
                    for b in range(2):
                        normalised(tile_of(xn, j * 2 + b), j * 2 + b).then_inc(xn_kept, 1)
                dve.wait_ge(logits_done, (r + 1) * TILES)
                steps.after(v.tensor_tensor(logits, bank[2][:, 0:TILES * E].rearrange("p (i e) -> p i e", e=E),
                                            router_bias[:].unsqueeze(1).to_broadcast([P, TILES, E]), ALU.add))
                steps.after(choose(r, logits, top1, 0))
                flat = "p i e -> p (i e)"
                steps.after(v.memset(ones, 1.0))
                steps.after(v.scalar_tensor_tensor(logits.rearrange(flat), eq.rearrange(flat), -BIG,
                                                   logits.rearrange(flat), ALU.mult, ALU.add))
                choose(r, logits, top2, 1).then_inc(hot_made, 1)
                v.tensor_tensor(weight2[:], top2, top1, ALU.subtract).then_inc(gap_made, 1)
                steps.after(v.memset(resume, 1.0))
                steps.after(v.memset(resume.rearrange("p (e j) -> p e j", e=E)[:, :, 0:1], 0.0))
                dve.wait_ge(counted, r + 1)
                steps.after(v.tensor_tensor_scan(taken, resume, bank[4][:], 0.0, ALU.mult, ALU.add))
                steps.after(v.tensor_tensor(taken, taken, bank[4][:], ALU.subtract))
                steps.after(v.tensor_tensor(taken, taken, bank[3][:], ALU.add))
                steps.after(v.tensor_tensor(taken, taken, hot, ALU.mult))
                steps.after(v.tensor_reduce(pos, taken.rearrange("p (e j) -> p j e", e=E), AX_X, ALU.add))
                steps.after(v.tensor_scalar(slot, rank12, -float(CAP), float(E * CAP), ALU.mult, ALU.add))
                steps.after(v.tensor_scalar(over, pos, float(CAP), float(SKIP), ALU.is_ge, ALU.mult))
                steps.after(v.tensor_tensor(over, over, slot, ALU.add))
                v.tensor_tensor(write_slot[:], over, pos, ALU.add).then_inc(slots_made, 1)
                steps.after(v.tensor_scalar(pos, pos, float(CAP - 1), None, ALU.min))
                steps.after(v.tensor_tensor(read_slot[:], pos, slot, ALU.add))
                dve.wait_ge(exp_made, r + 1)
                steps.after(v.tensor_scalar(weight1[:], weight2[:], 1.0, None, ALU.add))
                steps.after(v.reciprocal(weight1[:], weight1[:]))
                steps.after(v.scalar_tensor_tensor(weight2[:], weight2[:], 0.5, weight1[:], ALU.mult, ALU.mult))
                steps.after(v.tensor_scalar(weight1[:], weight1[:], 0.5, None, ALU.mult))

            def split_fc(done, k):
                raw, hi, lo = ((raw_fc, fc_hi, fc_lo), (raw_g, gw_hi, gw_lo))[k // 4]
                at = (slice(None), k % 4 // 2, slice(k % 2 * 512, k % 2 * 512 + 512))
                dve.wait_ge(fc_hi_made, done + k + 1)
                v.tensor_tensor(lo[at], raw[at], as_f32(hi[at]), ALU.subtract).then_inc(fc_split, 1)

            def expert(r, e, last):
                u = r * E + e

                def turned(n):
                    w, buf = GROUPS[n][1], n % 2
                    for kc in range(KC):
                        dve.wait_ge(xt_hi_made, (u * NG + n) * KC + kc + 1)
                        i = v.tensor_tensor(xt_lo[buf][:, kc, 0:w], bank[6 + kc][:, 0:w],
                                            as_f32(xt_hi[buf][:, kc, 0:w]), ALU.subtract)
                    i.then_inc(xt_split, 1)

                def product(unit):
                    w, b, col = GROUPS[unit // HJ][1], unit % 2, e * HJ + unit % HJ
                    dve.wait_ge(g_copied, u * UNITS + unit + 1)
                    if unit != 1:
                        dve.wait_ge(s_split, u * UNITS + max(unit - 1, 0))
                    v.scalar_tensor_tensor(hg[b][:, 0:w], bank[b][:, 0:w], bias_fc[:, bass.ds(col, 1)],
                                           g_sb[b][:, 0:w], ALU.add, ALU.mult).then_inc(hg_made, 1)

                def low(unit):
                    n, j, b = unit // HJ, unit % HJ, unit % 2
                    w, buf = GROUPS[n][1], n % 2
                    dve.wait_ge(s_hi_made, u * UNITS + unit + 1)
                    v.tensor_tensor(s_lo[buf][:, j, 0:w], hg[b][:, 0:w], as_f32(s_hi[buf][:, j, 0:w]),
                                    ALU.subtract).then_inc(s_split, 1)

                def project_low(k):
                    dve.wait_ge(proj_hi_made, u * 4 + k + 1)
                    at = (slice(None), slice(2 * k, 2 * k + 2), slice(None))
                    v.tensor_tensor(pr_lo[at], raw_proj[at], as_f32(pr_hi[at]), ALU.subtract).then_inc(proj_split, 1)

                def y_out(t):
                    n = t // 4 if t < 8 else 2
                    m = GROUP_TILES[n][t - 4 * n][1]
                    dve.wait_ge(y_done, u * Y_TILES + t + 1)
                    dve.wait_ge(y_stored[t % 2], (u * (Y_TILES // 2) + t // 2) * 16)
                    v.tensor_tensor(y_sb[0:m, t % 2, :], bank[4 + t % 2][0:m, 0:C], y_bias[0:m, :],
                                    ALU.add).then_inc(y_copied, 1)

                turned(0)
                v.tensor_scalar(bias_now[:], bias_g[:, bass.ds(e * HJ, HJ)], 1.0, None, ALU.mult
                                ).then_inc(bias_set, 1)
                dve.wait_ge(bias_loaded, u * 16 + 16)
                for unit in range(UNITS):
                    if unit % HJ == HJ // 2 and unit // HJ + 1 < NG:
                        turned(unit // HJ + 1)
                    if unit == 2 * HJ:
                        low(unit - 1)
                        for t in range(4):
                            y_out(t)
                    product(unit)
                    if unit and unit != 2 * HJ:
                        low(unit - 1)
                    if 2 <= unit < 6:
                        project_low(unit - 2)
                low(UNITS - 1)
                for t in range(4, Y_TILES):
                    if not last and t < 8:
                        split_fc(u * 8 + 8, 2 * (t - 4))
                        split_fc(u * 8 + 8, 2 * (t - 4) + 1)
                    y_out(t)

            def combine(r):
                with dve.Fori(0, TILES // RING) as o:
                    for b in range(RING):
                        i = o * RING + b
                        dve.wait_ge(rows_got[b], (r * (TILES // RING) + o + 1) * 32)
                        for k, w in enumerate((weight1, weight2)):
                            ins = v.scalar_tensor_tensor(tile_of(x, i), got[:, b, k, :], w[:, bass.ds(i, 1)],
                                                         tile_of(x, i), ALU.mult, ALU.add)
                            if k == 0:
                                ins.then_inc(row1_added, 1)
                                dve.wait_ge(row1_added, r * TILES + i + 1)
                            else:
                                ins.then_inc(combined, 1)

            def attention():
                for n, w in enumerate((wq, wk, wz, wv, wo)):
                    dve.wait_ge(aw_hi_made, n + 1)
                    v.tensor_tensor(w[1].rearrange("p a n -> p (a n)"), raw_w,
                                    as_f32(w[0].rearrange("p a n -> p (a n)")), ALU.subtract).then_inc(aw_split, 1)
                combine(0)
                dve.wait_ge(combined, TILES)
                with dve.Fori(0, TILES) as i:
                    tile_stats(i).then_inc(stats_made, 1)
                inverse_deviation(2)
                dve.wait_ge(aw_split, 5)
                v.memset(state, 0.0).then_inc(att_cleared, 1)
                v.memset(near[:, :, HALF - 1:HALF], 1.0).then_inc(att_cleared, 1)
                for h in range(2):
                    v.memset(prob[h][HALF:P, :, 0:HALF], 0.0).then_inc(att_cleared, 1)
                dve.wait_ge(att_cleared, ATT_CLEARS)

                def supertile(s):
                    dve.wait_ge(xna_turned, s)
                    for b in range(SUPER):
                        normalised(xna[:, b, :], s * SUPER + b).then_inc(xna_made, 1)
                    for kc in range(KC):
                        dve.wait_ge(xa_hi_made, s * KC + kc + 1)
                        v.tensor_tensor(xa[1][:, kc, :], bank[3 + kc][:], as_f32(xa[0][:, kc, :]),
                                        ALU.subtract).then_inc(xa_split, 1)
                    lower, upper = slice(0, HALF), slice(HALF, P)

                    def prepare(g):
                        G = s * NPAIR + g
                        dve.wait_ge(decay_made, G + 1)
                        for c in range(SUPER):
                            v.tensor_tensor_scan(near[:, c, HALF - 2::-1], decay[:, c, HALF - 1:0:-1],
                                                 zeros[:, 0:HALF - 1], 1.0, ALU.mult, ALU.add
                                                 ).then_inc(dve_steps, 1)
                            steps.n += 1
                            v.tensor_tensor_scan(near[:, c, upper], decay[:, c, upper], zeros[:], 1.0,
                                                 ALU.mult, ALU.add).then_inc(dve_steps, 1)
                            steps.n += 1
                        dve.wait_ge(dve_steps, steps.base + steps.n)
                        steps.after(v.tensor_scalar(far, near, TINY, None, ALU.max))
                        steps.after(v.reciprocal(far, far))
                        steps.after(v.tensor_tensor(enter[:], decay[:, :, 0], near[:, :, 0], ALU.mult))
                        steps.after(v.tensor_copy(carry[:], enter[:]))
                        steps.after(v.tensor_tensor(carry[:, 1:SUPER], enter[:, 1:SUPER], near[:, 0:SUPER - 1, P - 1],
                                                    ALU.mult))
                        dve.wait_ge(qk_done, G + 1)
                        bq, bk = (bank[n][:].rearrange("p (a n) -> p a n", n=P) for n in (0, 1))
                        q = qd[g % 2]
                        for o, i, w, part_ in ((q, bq, far, lower), (q, bq, near, upper),
                                               (kd, bk, near, lower), (kd, bk, far, upper)):
                            ins = v.tensor_tensor(o[:, :, part_], i[:, :, part_], w[:, :, part_], ALU.mult)
                        ins.then_inc(qk_made, 1)

                    prepare(0)
                    for g in range(NPAIR):
                        G = s * NPAIR + g
                        dve.wait_ge(scores_done, G + 1)
                        for h in range(2):
                            sc = bank[3 + h][:].rearrange("p (a n) -> p a n", n=P)
                            v.tensor_tensor(prob[h][lower, :, :], sc[lower, :, :],
                                            causal[lower, :].unsqueeze(1).to_broadcast([HALF, SUPER, P]), ALU.mult)
                            ins = v.tensor_tensor(prob[h][upper, :, upper], sc[upper, :, upper],
                                                  causal[upper, upper].unsqueeze(1).to_broadcast([HALF, SUPER, HALF]),
                                                  ALU.mult)
                        ins.then_inc(prob_made, 1)
                        dve.wait_ge(kv_done, G + 1)
                        for c in range(SUPER):
                            src = state[:, g, :] if c == 0 else state_sum[:]
                            two = "p (h n) -> p h n"
                            v.scalar_tensor_tensor(state_in[:, c, :].rearrange(two, h=2), src.rearrange(two, h=2),
                                                   carry[:, c:c + 1],
                                                   head_of[:].unsqueeze(2).to_broadcast([P, 2, DH]),
                                                   ALU.mult, ALU.mult).then_inc(state_ready, 1)
                            dve.wait_ge(state_ready, G * SUPER + c + 1)
                            steps.after(v.tensor_tensor(state_sum[:], bank[7][:, c * P:(c + 1) * P],
                                                        state_in[:, c, :], ALU.add))
                        v.tensor_scalar(state[:, g, :], state_sum[:], near[:, SUPER - 1, P - 1:P], None,
                                        ALU.mult).then_inc(state_kept, 1)
                        dve.wait_ge(state_kept, G + 1)
                        if g + 1 < NPAIR:
                            prepare(g + 1)
                        dve.wait_ge(ot_hi_made, G + 1)
                        v.tensor_tensor(ot[1][:, g, :], bank[5][:], as_f32(ot[0][:, g, :]),
                                        ALU.subtract).then_inc(ot_split, 1)
                    for b in range(SUPER):
                        i = s * SUPER + b
                        dve.wait_ge(wo_done, i + 1)
                        v.tensor_tensor(tile_of(x, i), bank[3 + b % 2][:, 0:C], tile_of(x, i),
                                        ALU.add).then_inc(wo_added, 1)
                    for b in range(SUPER):
                        i = s * SUPER + b
                        dve.wait_ge(wo_added, i + 1)
                        dve.sem_inc(x_settled, 1)
                        tile_stats(i).then_inc(stats_made, 1)

                steps.loop(0, NSUP, NPAIR * (2 * SUPER + 5 + SUPER), supertile)

            for i in range(4):
                dve.wait_ge(x_loaded[i], 16)
                with dve.Fori(i * TILES // 4, (i + 1) * TILES // 4) as t:
                    tile_stats(t).then_inc(stats_made, 1)
            for r in range(2):
                inverse_deviation(2 * r + 1)
                route(r)
                for k in range(8):
                    split_fc(r * E * 8, k)
                with dve.Fori(0, E - 1) as e:
                    expert(r, e, False)
                expert(r, E - 1, True)
                if r == 0:
                    attention()
            combine(1)


_INS = ["L0_attn_x", "L0_attn_W_q", "L0_attn_W_k", "L0_attn_W_v", "L0_attn_W_gate", "L0_attn_b_gate",
        "L0_attn_W_o", "L0_ffn_router_w", "L0_ffn_router_b", "L0_ffn_w_c_fc", "L0_ffn_b_c_fc",
        "L0_ffn_w_gate", "L0_ffn_b_gate", "L0_ffn_w_c_proj", "L0_ffn_b_c_proj"]


def kernel(**inputs):
    import numpy as _np
    import concourse.bacc as _bacc
    from concourse.bass_utils import run_bass_kernel_spmd as _run

    nc = _bacc.Bacc("TRN2", target_bir_lowering=False, num_devices=1)
    arrays, args = {}, []
    for name in _INS:
        a = _np.ascontiguousarray(inputs[name])
        arrays[f"in_{name}"] = a
        args.append(nc.dram_tensor(f"in_{name}", a.shape, mybir.dt.from_np(a.dtype), kind="ExternalInput").ap())
    args.append(nc.dram_tensor("out_x", (1, T, C), F32, kind="ExternalOutput").ap())
    macaron(nc, *args)
    r = _run(nc, [arrays], core_ids=[0])
    return r.results[0]["out_x"]
```

```python
from contextlib import ExitStack

import concourse.bass as bass
from concourse import mybir

ALU = mybir.AluOpType
ACT = mybir.ActivationFunctionType
AX_X = mybir.AxisListType.X
F32 = mybir.dt.float32
F32R = mybir.dt.float32r
BF16 = mybir.dt.bfloat16
U32 = mybir.dt.uint32

P = 128
T = 4096
C = 256
KC = C // P
TILES = T // P
EPS = 1e-5

E = 8
TOPK = 2
HID = 1024
HJ = HID // P
CAP = int(1.2 * TOPK * T // E)
ROWS = E * CAP
PICKS = TOPK * TILES
SKIP = 1 << 17
BIG = 1e30
GROUPS = [(s, min(512, CAP - s)) for s in range(0, CAP, 512)]
GROUP_TILES = [[(o, min(P, n - o)) for o in range(0, n, P)] for _, n in GROUPS]
Y_TILES = sum(len(t) for t in GROUP_TILES)
NG = len(GROUPS)
UNITS = NG * HJ

HEADS = 16
DH = 64
NPAIR = HEADS * DH // P
SUPER = 4
NSUP = TILES // SUPER
QUARTERS = 4
QT = TILES // QUARTERS
SW = SUPER * P
HALF = P // 2
LIMIT = 80.0

BLOCKS = [(0, q * QT, QT) for q in range(QUARTERS)] + [(1, 0, TILES)]

CLEAR_ROWS = 8
CLEAR = CLEAR_ROWS * P
CLEARS = -(-ROWS // CLEAR)
CONSTS = 7
ATT_CLEARS = 5
RING = 16
assert ROWS % CLEAR_ROWS == 0 and NG == 3 and Y_TILES % 2 == 0


class Steps:

    def __init__(self, eng, sem):
        self.eng, self.sem, self.base, self.n = eng, sem, 0, 0

    def after(self, ins):
        ins.then_inc(self.sem, 1)
        self.n += 1
        self.eng.wait_ge(self.sem, self.base + self.n)

    def loop(self, lo, hi, per, body):
        start = self.base + self.n
        with self.eng.Fori(lo, hi) as i:
            self.base, self.n = start + (i - lo) * per, 0
            body(i)
            assert self.n == per, (self.n, per)
        self.base, self.n = start + (hi - lo) * per, 0


def macaron(nc, x_in, w_q, w_k, w_v, w_gate, b_gate, w_o, router_w, router_b,
            w_fc, b_fc, w_g, b_g, w_proj, b_proj, out):
    with ExitStack() as ctx:
        def sb(name, shape, dt=F32):
            return ctx.enter_context(nc.sbuf_tensor(name, shape, dt))

        def sem(name):
            return ctx.enter_context(nc.semaphore(name))

        expert_in = nc.dram_tensor("expert_in", (ROWS, C), F32, kind="Internal").ap()
        expert_out = nc.dram_tensor("expert_out", (ROWS, C), F32, kind="Internal").ap()

        x = sb("x", [P, TILES, C])
        wide = sb("wide", [P, 8192])
        temp = sb("temp", [P, 2048])
        rows = sb("rows", [P, 1024])
        halves = sb("halves", [P, 32768], F32R)
        ident = sb("ident", [P, P])
        causal = sb("causal", [P, P], BF16)
        before = sb("before", [P, P], BF16)
        head_of = sb("head_of", [P, 2])
        limit = sb("limit", [P, HALF], BF16)
        rank = sb("rank", [P, E])
        router = sb("router", [P, KC, E])
        router_bias = sb("router_bias", [P, E])
        rstd = sb("rstd", [P, TILES])
        read_slot = sb("read_slot", [P, PICKS], U32)
        weight1 = sb("weight1", [P, TILES])
        weight2 = sb("weight2", [P, TILES])
        bias_fc = sb("bias_fc", [P, E * HJ])
        bias_g = sb("bias_g", [P, E * HJ])
        bias_gate = sb("bias_gate", [P, NPAIR])
        stats = sb("stats", [P, TILES, 6])
        bias_now = sb("bias_now", [P, HJ])
        carry = sb("carry", [P, 2, SUPER])
        leave = sb("leave", [P, 2])
        state_sum = sb("state_sum", [P, P])
        long = sb("long", [1, E], U32)

        def part(t, at, *dims):
            n = 1
            for d in dims:
                n *= d
            v = t[:, at:at + n]
            names = "abc"[:len(dims)]
            if len(dims) == 1:
                return v
            return v.rearrange(f"p ({' '.join(names)}) -> p {' '.join(names)}",
                               **{names[i]: dims[i] for i in range(1, len(dims))})

        xn = part(wide, 0, TILES, C)
        raw_fc = part(wide, 0, KC, HID)
        raw_g = part(wide, 2048, KC, HID)
        raw_proj = part(wide, 4096, HJ, C)
        xg = [part(wide, 6144, 4, C), part(wide, 7168, 4, C)]
        got = part(wide, 0, RING, TOPK, C)
        g_sb = [part(temp, 0, 512), part(temp, 512, 512)]
        hg = [part(temp, 1024, 512), part(temp, 1536, 512)]
        y_sb = part(rows, 0, 2, C)
        y_bias = part(rows, 512, C)
        fc_hi, fc_lo, gw_hi, gw_lo = (part(halves, 2048 * i, KC, HID) for i in range(4))
        pr_hi, pr_lo = (part(halves, 2048 * i, HJ, C) for i in (4, 5))
        s_hi = [part(halves, 12288 + 8192 * i, HJ, 512) for i in range(2)]
        s_lo = [part(halves, 16384 + 8192 * i, HJ, 512) for i in range(2)]
        xt_hi = [part(halves, 28672 + 2048 * i, KC, 512) for i in range(2)]
        xt_lo = [part(halves, 29696 + 2048 * i, KC, 512) for i in range(2)]
        xnt = [part(rows, 0, KC, SW), part(temp, 0, KC, SW)]
        taken = part(temp, 1024, 256)
        hot = part(temp, 1280, 256).bitcast(BF16)
        resume = part(temp, 1536, 128).bitcast(BF16)
        logits = part(temp, 1664, QT, E)
        chosen = part(temp, 1728, QT, E)
        pos = part(temp, 1792, PICKS)
        best = part(temp, 1856, PICKS)
        write_slot = part(temp, 1920, PICKS).bitcast(U32)
        top = [part(temp, 1984, QT), part(temp, 1992, QT)]
        given = [part(temp, 2000, E), part(temp, 2008, E)]
        first_slot = part(temp, 2016, TILES)
        ones = part(state_sum, 0, P // 2).bitcast(BF16)
        over = part(state_sum, P // 2, TILES)
        v_sb = part(wide, 0, SUPER, HEADS * DH)
        near = part(wide, 4096, SUPER, 2 * (HALF + 1)).rearrange("p a (h n) -> p a h n", h=2)
        far = part(wide, 4616, SUPER, 2 * (HALF + 1)).rearrange("p a (h n) -> p a h n", h=2)
        qd = [part(wide, 5136, SUPER, P), part(wide, 5648, SUPER, P)]
        kd = part(wide, 6160, SUPER, P)
        prob = [part(wide, 6672, SUPER, P), part(wide, 7184, SUPER, P)]
        stats_now = part(wide, 7696, SUPER, 6)
        mean_now, var_now, rstd_now = (part(wide, 7720 + SUPER * i, SUPER) for i in range(3))
        kdt = part(temp, 0, SUPER, P)
        state_in = part(temp, 512, SUPER, P)
        state = part(temp, 1024, NPAIR, P)
        xna = part(rows, 0, SUPER, C)
        raw_w = [part(wide, 2048 * i, 2048) for i in range(4)] + [part(temp, 0, 2048)]
        wq, wk, wz, wv = ([part(halves, 4096 * i, KC, 1024), part(halves, 4096 * i + 2048, KC, 1024)]
                          for i in range(4))
        wo = [part(halves, 16384, NPAIR, C), part(halves, 18432, NPAIR, C)]
        xa = [part(halves, 20480, KC, SW), part(halves, 21504, KC, SW)]
        ot = [part(halves, 22528, NPAIR, SW), part(halves, 26624, NPAIR, SW)]
        got4 = part(halves, 30720, SUPER, TOPK, C).bitcast(F32)

        bank = [ctx.enter_context(nc.psum_tensor(f"bank{i}", [P, 512], F32)) for i in range(8)]

        x_loaded = [sem(f"x_loaded{i}") for i in range(4)]
        small_loaded = sem("small_loaded")
        consts_made = sem("consts_made")
        pool_steps = sem("pool_steps")
        zero_made = sem("zero_made")
        cleared = sem("cleared")
        bias_turned, bias_set = sem("bias_turned"), sem("bias_set")
        stats_made, x_settled = sem("stats_made"), sem("x_settled")
        dve_steps = sem("dve_steps")
        act_steps = sem("act_steps")
        var_made = sem("var_made")
        std_made = sem("std_made")
        xn_made = sem("xn_made")
        xn_turned = sem("xn_turned")
        xnt_copied = sem("xnt_copied")
        logits_done = sem("logits_done")
        gap_made = sem("gap_made")
        exp_made = sem("exp_made")
        hot_made = [sem("hot_made0"), sem("hot_made1")]
        counted, long_made = sem("counted"), sem("long_made")
        slots_made = sem("slots_made")
        scattered = [sem(f"scattered{i}") for i in range(4)]
        fc_staged = sem("fc_staged")
        proj_staged = sem("proj_staged")
        fc_hi_made, fc_split = sem("fc_hi_made"), sem("fc_split")
        proj_hi_made, proj_split = sem("proj_hi_made"), sem("proj_split")
        bias_loaded = sem("bias_loaded")
        xg_loaded = [sem("xg_loaded0"), sem("xg_loaded1")]
        xg_turned = sem("xg_turned")
        xt_hi_made, xt_split = sem("xt_hi_made"), sem("xt_split")
        up_done = sem("up_done")
        g_copied = sem("g_copied")
        hg_made = sem("hg_made")
        silu_made = sem("silu_made")
        s_hi_made, s_split = sem("s_hi_made"), sem("s_split")
        y_done = sem("y_done")
        y_copied = sem("y_copied")
        y_stored = [sem("y_stored0"), sem("y_stored1")]
        rows_got = [sem(f"rows_got{i}") for i in range(RING)]
        row1_added, combined = sem("row1_added"), sem("combined")
        aw_staged = [sem(f"aw_staged{i}") for i in range(5)]
        aw_hi_made, aw_split = sem("aw_hi_made"), sem("aw_split")
        stats4_made, var4_made, std4_made = sem("stats4_made"), sem("var4_made"), sem("std4_made")
        att_cleared = sem("att_cleared")
        xna_made, xna_turned = sem("xna_made"), sem("xna_turned")
        xa_hi_made, xa_split = sem("xa_hi_made"), sem("xa_split")
        z_done, qk_done = sem("z_done"), sem("qk_done")
        z_used, log_made, log_summed = sem("z_used"), sem("log_made"), sem("log_summed")
        near_made, far_made, qk_made = sem("near_made"), sem("far_made"), sem("qk_made")
        v_done, v_copied = sem("v_done"), sem("v_copied")
        k_turned, kdt_copied = sem("k_turned"), sem("kdt_copied")
        scores_done, prob_made = sem("scores_done"), sem("prob_made")
        kv_done, state_ready, state_kept = sem("kv_done"), sem("state_ready"), sem("state_kept")
        o_done, ot_hi_made, ot_split = sem("o_done"), sem("ot_hi_made"), sem("ot_split")
        wo_done, wo_added = sem("wo_done"), sem("wo_added")
        stored = sem("stored")

        block = ctx.enter_context(nc.Block())

        def as_f32(ap):
            return ap.bitcast(F32)

        def has_last_group(eng, e):
            return eng.value_load(long[0:1, bass.ds(e, 1)], min_val=0, max_val=1)

        def passes(hi_lo_a, hi_lo_b):
            (ah, al), (bh, bl) = hi_lo_a, hi_lo_b
            return [(ah, bh), (ah, bl), (al, bh)]

        tok = "(i p) c -> p i c"

        @block.sync
        def _(sp):
            sp.dma_start(router[:], router_w.rearrange("(a p) e -> p a e", p=P)).then_inc(small_loaded, 16)
            sp.dma_start(router_bias[:], router_b.rearrange("(a e) -> a e", a=1).to_broadcast([P, E])).then_inc(small_loaded, 16)
            sp.dma_start(rows[0:E * HJ, 0:P], b_fc.rearrange("e a (j p) -> (e a j) p", p=P)).then_inc(small_loaded, 16)
            sp.dma_start(rows[0:E * HJ, P:2 * P], b_g.rearrange("e a (j p) -> (e a j) p", p=P)).then_inc(small_loaded, 16)
            sp.dma_start(rows[0:NPAIR, 2 * P:3 * P], b_gate.rearrange("(j p) -> j p", p=P)).then_inc(small_loaded, 16)
            for i in range(4):
                n = TILES // 4
                sp.dma_start(x[:, i * n:(i + 1) * n, :],
                             x_in[0, i * n * P:(i + 1) * n * P, :].rearrange(tok, p=P)).then_inc(x_loaded[i], 16)
            sp.wait_ge(zero_made, 1)
            for at in range(0, ROWS, CLEAR):
                n = min(CLEAR, ROWS - at) // CLEAR_ROWS
                sp.dma_start(expert_in[at:at + n * CLEAR_ROWS, :].rearrange("(p a) c -> p (a c)", a=CLEAR_ROWS),
                             as_f32(halves[0:n, 0:CLEAR_ROWS * C])).then_inc(cleared, 16)

            def load_rows(r, e, n):
                u = r * E + e
                sp.wait_ge(xg_turned, [u * NG, u * NG, u * NG + 1][n])
                buf = n % 2
                s, m = GROUPS[n]
                full = m // P
                at = e * CAP + s
                sp.dma_start(xg[buf][:, 0:full, :],
                             expert_in[bass.ds(at, full * P), :].rearrange(tok, p=P)).then_inc(xg_loaded[buf], 16)
                if m % P:
                    sp.dma_start(xg[buf][0:m % P, full, :],
                                 expert_in[bass.ds(at + full * P, m % P), :]).then_inc(xg_loaded[buf], 16)

            def stage_fc(r, e):
                sp.wait_ge(fc_split, (r * E + e) * 8)
                sp.dma_start(raw_fc, w_fc[e].rearrange("(a p) n -> p a n", p=P)).then_inc(fc_staged, 16)
                sp.dma_start(raw_g, w_g[e].rearrange("(a p) n -> p a n", p=P)).then_inc(fc_staged, 16)

            def stage_proj(r, e):
                sp.wait_ge(proj_split, (r * E + e) * 4)
                sp.dma_start(raw_proj, w_proj[e].rearrange("(a p) n -> p a n", p=P)).then_inc(proj_staged, 16)

            def load_bias(r, e):
                sp.dma_start(y_bias, b_proj[e].to_broadcast([P, C])).then_inc(bias_loaded, 16)

            def store_y(r, e, t):
                u = r * E + e
                sp.wait_ge(y_copied, u * Y_TILES + t + 1)
                n = t // 4 if t < 8 else 2
                o, m = GROUP_TILES[n][t - 4 * n]
                at = e * CAP + GROUPS[n][0] + o
                sp.dma_start(expert_out[bass.ds(at, m), :], y_sb[0:m, t % 2, :]).then_inc(y_stored[t % 2], 16)

            def stage_attention(n, *producer):
                w = (w_q, w_k, w_gate, w_v, w_o)[n]
                sp.wait_ge(*producer)
                sp.dma_start(raw_w[n].rearrange("p (a n) -> p a n", a=w.shape[0] // P),
                             w.rearrange("(a p) n -> p a n", p=P)).then_inc(aw_staged[n], 16)

            def expert(r, e, last):
                load_rows(r, e, 2)
                if not last:
                    stage_fc(r, e + 1)
                    stage_proj(r, e + 1)
                elif r == 0:
                    stage_attention(0, fc_split, E * 8)
                    stage_attention(1, fc_split, E * 8)
                    stage_attention(2, proj_split, E * 4)
                    stage_attention(3, xg_turned, E * NG)
                for t in range(4):
                    store_y(r, e, t)
                if not last:
                    load_rows(r, e + 1, 0)
                    load_rows(r, e + 1, 1)
                elif r == 0:
                    stage_attention(4, s_split, E * UNITS)
                for t in range(4, Y_TILES):
                    store_y(r, e, t)
                if not last:
                    load_bias(r, e + 1)

            for r in range(2):
                quarter = (r + 1) * TOPK * QT * 16
                sp.wait_ge(scattered[0], quarter)
                sp.wait_ge(scattered[1], quarter)
                stage_fc(r, 0)
                sp.wait_ge(scattered[2], quarter)
                stage_proj(r, 0)
                sp.wait_ge(scattered[3], quarter)
                load_rows(r, 0, 0)
                load_rows(r, 0, 1)
                load_bias(r, 0)
                with sp.Fori(0, E - 1) as e:
                    expert(r, e, False)
                expert(r, E - 1, True)
            with sp.Fori(0, TILES) as i:
                sp.wait_ge(combined, TILES + i + 1)
                sp.dma_start(out[0, bass.ds(i * P, P), :], x[:, bass.ds(i, 1), :].rearrange("p a c -> p (a c)")).then_inc(stored, 16)
            sp.wait_ge(stored, TILES * 16)

        @block.gpsimd
        def _(pool):
            steps = Steps(pool, pool_steps)
            steps.after(nc.gpsimd.memset(ident[:], 0.0))
            steps.after(nc.gpsimd.memset(causal[:], 1.0))
            steps.after(nc.gpsimd.memset(before[:], 1.0))
            steps.after(nc.gpsimd.memset(head_of[:], 1.0))
            nc.gpsimd.affine_select(out=ident[:], in_=ident[:], compare_op=ALU.not_equal, fill=1.0, base=0,
                                    pattern=[[-1, P]], channel_multiplier=1).then_inc(consts_made, 1)
            nc.gpsimd.affine_select(out=causal[:], in_=causal[:], compare_op=ALU.is_ge, fill=0.0, base=0,
                                    pattern=[[1, P]], channel_multiplier=-1).then_inc(consts_made, 1)
            nc.gpsimd.affine_select(out=before[:], in_=before[:], compare_op=ALU.is_gt, fill=0.0, base=0,
                                    pattern=[[1, P]], channel_multiplier=-1).then_inc(consts_made, 1)
            nc.gpsimd.affine_select(out=head_of[:, 0:1], in_=head_of[:, 0:1], compare_op=ALU.is_ge, fill=0.0,
                                    base=DH - 1, pattern=[[0, 1]], channel_multiplier=-1).then_inc(consts_made, 1)
            nc.gpsimd.affine_select(out=head_of[:, 1:2], in_=head_of[:, 1:2], compare_op=ALU.is_ge, fill=0.0,
                                    base=-DH, pattern=[[0, 1]], channel_multiplier=1).then_inc(consts_made, 1)
            nc.gpsimd.memset(limit[:], LIMIT).then_inc(consts_made, 1)
            nc.gpsimd.iota(rank[:], [[-1, E]], base=E, channel_multiplier=0,
                           allow_small_or_imprecise_dtypes=True).then_inc(consts_made, 1)
            for r in range(2):
                for n, (k, first, tiles) in enumerate(BLOCKS):
                    pool.wait_ge(slots_made, r * len(BLOCKS) + n + 1)
                    if r == 0 and n == 0:
                        pool.wait_ge(cleared, CLEARS * 16)
                    for i in range(first, first + tiles):
                        j = k * TILES + i
                        pool.indirect_dma_start(expert_in,
                                                bass.IndirectOffsetOnAxis(ap=write_slot[:, j:j + 1], axis=0),
                                                xn[:, i, :], None, bounds_check=ROWS - 1,
                                                oob_is_err=False).then_inc(scattered[i // QT], 16)
                for b in range(2):
                    pool.wait_ge(y_stored[b], (r + 1) * E * Y_TILES // 2 * 16)
                ring, buffers = (SUPER, got4) if r == 0 else (RING, got)
                for i in range(TILES):
                    if i >= ring:
                        pool.wait_ge(combined, r * TILES + i - ring + 1)
                    for k in range(TOPK):
                        j = k * TILES + i
                        pool.indirect_dma_start(buffers[:, i % ring, k, :], None, expert_out,
                                                bass.IndirectOffsetOnAxis(ap=read_slot[:, j:j + 1], axis=0)
                                                ).then_inc(rows_got[i % ring], 16)

        @block.tensor
        def _(pe):
            pe.wait_ge(consts_made, CONSTS)
            pe.wait_ge(small_loaded, 16 * 5)
            for n, (k, at) in enumerate(((E * HJ, 0), (E * HJ, P), (NPAIR, 2 * P))):
                pe.transpose(bank[n][:, 0:k], rows[0:k, at:at + P], ident[0:k, 0:k]).then_inc(bias_turned, 1)

            def route(r):
                def turn_xn(s):
                    pe.wait_ge(xn_made, (r * NSUP + s + 1) * SUPER)
                    for kc in range(KC):
                        for b in range(SUPER):
                            m = pe.transpose(bank[6 * (s % 2) + kc][:, b * P:(b + 1) * P],
                                             xn[:, s * SUPER + b, kc * P:(kc + 1) * P], ident[:])
                    m.then_inc(xn_turned, 1)

                def count(n):
                    k, first, tiles = BLOCKS[n]
                    cols = slice((k * TILES + first) * E, (k * TILES + first + tiles) * E)
                    pe.wait_ge(hot_made[k], r * QUARTERS + (QUARTERS if k else n + 1))
                    if n:
                        pe.wait_ge(slots_made, r * len(BLOCKS) + n)
                    pe.matmul(bank[3][:, cols], before[:], hot[:, cols], start=True, stop=True)
                    pe.matmul(bank[4][:, cols], ones, hot[:, cols], start=True, stop=True).then_inc(counted, 1)

                turn_xn(0)
                for s in range(NSUP):
                    if s + 1 < NSUP:
                        turn_xn(s + 1)
                    pe.wait_ge(xnt_copied, (r * NSUP + s + 1) * KC)
                    for b in range(SUPER):
                        i = s * SUPER + b
                        for kc in range(KC):
                            m = pe.matmul(bank[(2, 5)[i // QT % 2]][:, i * E:(i + 1) * E], xnt[s % 2][:, kc, b * P:(b + 1) * P],
                                          router[:, kc, :], start=(kc == 0), stop=(kc == KC - 1))
                    m.then_inc(logits_done, 1)
                    if s > 1 and s % 2:
                        count(s // 2 - 1)
                count(QUARTERS - 1)
                count(QUARTERS)

            def turn(r, e, n):
                u = r * E + e
                buf = n % 2
                pe.wait_ge(xg_loaded[buf], [u * 48 + 16, u * 16 + 16, u * 48 + 48][n])
                pe.wait_ge(xt_split, u * NG + n)
                for kc in range(KC):
                    for i, (o, m) in enumerate(GROUP_TILES[n]):
                        t = pe.transpose(bank[6 + kc][:, o:o + m], xg[buf][0:m, i, kc * P:(kc + 1) * P],
                                         ident[0:m, 0:m])
                t.then_inc(xg_turned, 1)

            def up(r, e, n, js):
                u = r * E + e
                buf, w = n % 2, GROUPS[n][1]
                if js[0] == 0:
                    pe.wait_ge(xt_split, u * NG + n + 1)
                    if n == 0:
                        pe.wait_ge(fc_split, u * 8 + 8)
                for j in js:
                    unit = n * HJ + j
                    b = unit % 2
                    if unit >= 2:
                        pe.wait_ge(hg_made, u * UNITS + unit - 1)
                    for at, hi_lo in ((0, (fc_hi, fc_lo)), (2, (gw_hi, gw_lo))):
                        ps = [(kc, a, v) for kc in range(KC) for a, v in passes(hi_lo, (xt_hi[buf], xt_lo[buf]))]
                        for i, (kc, a, v) in enumerate(ps):
                            m = pe.matmul(bank[at + b][:, 0:w], a[:, kc, j * P:(j + 1) * P], v[:, kc, 0:w],
                                          start=(i == 0), stop=(i == len(ps) - 1))
                    m.then_inc(up_done, 1)

            def down(r, e, n):
                u = r * E + e
                buf = n % 2
                pe.wait_ge(s_split, u * UNITS + (n + 1) * HJ)
                if n == 0:
                    pe.wait_ge(proj_split, u * 4 + 4)
                for i, (o, m) in enumerate(GROUP_TILES[n]):
                    t = 4 * n + i
                    if t >= 2:
                        pe.wait_ge(y_copied, u * Y_TILES + t - 1)
                    ps = [(j, a, v) for j in range(HJ)
                          for a, v in passes((s_hi[buf], s_lo[buf]), (pr_hi, pr_lo))]
                    for k, (j, a, v) in enumerate(ps):
                        mm = pe.matmul(bank[4 + t % 2][0:m, 0:C], a[:, j, o:o + m], v[:, j, :],
                                       start=(k == 0), stop=(k == len(ps) - 1))
                    mm.then_inc(y_done, 1)

            def expert(r, e, last):
                first, second = range(HJ // 2), range(HJ // 2, HJ)
                up(r, e, 0, first)
                turn(r, e, 1)
                up(r, e, 0, second)
                up(r, e, 1, first)
                turn(r, e, 2)
                up(r, e, 1, second)
                down(r, e, 0)
                last_group = has_last_group(pe, e)
                with pe.If(last_group):
                    up(r, e, 2, range(HJ))
                with pe.Else():
                    pe.drain().then_inc(up_done, HJ)
                down(r, e, 1)
                if not last:
                    turn(r, e + 1, 0)
                with pe.If(last_group):
                    down(r, e, 2)
                with pe.Else():
                    pe.drain().then_inc(y_done, len(GROUP_TILES[2]))

            def attention():
                def turn_x(s):
                    pe.wait_ge(xna_made, s * SUPER + SUPER)
                    for kc in range(KC):
                        for b in range(SUPER):
                            m = pe.transpose(bank[kc][:, b * P:(b + 1) * P], xna[:, b, kc * P:(kc + 1) * P], ident[:])
                    m.then_inc(xna_turned, 1)

                def project(at, w, g):
                    ps = [(kc, a, v) for kc in range(KC) for a, v in passes(w, xa)]
                    for i, (kc, a, v) in enumerate(ps):
                        m = pe.matmul(bank[at][:], a[:, kc, g * P:(g + 1) * P], v[:, kc, :],
                                      start=(i == 0), stop=(i == len(ps) - 1))
                    return m

                def project_z(s, g):
                    project(2, wz, g).then_inc(z_done, 1)

                def project_qk(s, g):
                    project(0, wq, g)
                    project(1, wk, g).then_inc(qk_done, 1)

                def values(s):
                    for b in range(SUPER):
                        for half in range(2):
                            n = 2 * b + half
                            if n >= 2:
                                pe.wait_ge(v_copied, s * 8 + n - 1)
                            ps = [(kc, a, v) for kc in range(KC) for a, v in passes(xa, wv)]
                            for i, (kc, a, v) in enumerate(ps):
                                m = pe.matmul(bank[5 + n % 2][:], a[:, kc, b * P:(b + 1) * P],
                                              v[:, kc, half * 512:(half + 1) * 512],
                                              start=(i == 0), stop=(i == len(ps) - 1))
                            m.then_inc(v_done, 1)
                    pe.wait_ge(v_copied, s * 8 + 8)

                def scores(s, g):
                    G = s * NPAIR + g
                    pe.wait_ge(qk_made, G + 1)
                    for c in range(SUPER):
                        m = pe.transpose(bank[6][:, c * P:(c + 1) * P], kd[:, c, :], ident[:])
                    m.then_inc(k_turned, 1)
                    if g:
                        pe.wait_ge(prob_made, G)
                    for c in range(SUPER):
                        for h in range(2):
                            hp = slice(h * DH, (h + 1) * DH)
                            m = pe.matmul(bank[3 + h][:, c * P:(c + 1) * P], kd[hp, c, :], qd[g % 2][hp, c, :],
                                          start=True, stop=True)
                    m.then_inc(scores_done, 1)

                def additions(s, g):
                    G = s * NPAIR + g
                    pe.wait_ge(kdt_copied, G + 1)
                    if g:
                        pe.wait_ge(state_kept, G)
                    for c in range(SUPER):
                        m = pe.matmul(bank[7][:, c * P:(c + 1) * P], kdt[:, c, :], v_sb[:, c, g * P:(g + 1) * P],
                                      start=True, stop=True)
                    m.then_inc(kv_done, 1)

                def outputs(s, g):
                    G = s * NPAIR + g
                    pe.wait_ge(prob_made, G + 1)
                    if g:
                        pe.wait_ge(ot_split, G)
                    for c in range(SUPER):
                        pe.wait_ge(state_ready, G * SUPER + c + 1)
                        cols = slice(c * P, (c + 1) * P)
                        pe.matmul(bank[5][:, cols], state_in[:, c, :], qd[g % 2][:, c, :],
                                  start=True, stop=False, skip_group_check=True)
                        for h in range(2):
                            m = pe.matmul(bank[5][h * DH:(h + 1) * DH, cols],
                                          v_sb[:, c, g * P + h * DH:g * P + (h + 1) * DH], prob[h][:, c, :],
                                          start=False, stop=True, skip_group_check=True)
                    m.then_inc(o_done, 1)

                def out_projection(s):
                    pe.wait_ge(ot_split, s * NPAIR + NPAIR)
                    for b in range(SUPER):
                        if b >= 2:
                            pe.wait_ge(wo_added, s * SUPER + b - 1)
                        ps = [(g, a, v) for g in range(NPAIR) for a, v in passes(ot, wo)]
                        for i, (g, a, v) in enumerate(ps):
                            m = pe.matmul(bank[3 + b % 2][:, 0:C], a[:, g, b * P:(b + 1) * P], v[:, g, :],
                                          start=(i == 0), stop=(i == len(ps) - 1))
                        m.then_inc(wo_done, 1)

                def supertile(s, last):
                    for g in range(NPAIR):
                        G = s * NPAIR + g
                        if g + 1 < NPAIR:
                            pe.wait_ge(z_used, G + 1)
                            project_z(s, g + 1)
                        scores(s, g)
                        if g:
                            outputs(s, g - 1)
                        additions(s, g)
                        if g + 1 < NPAIR:
                            project_qk(s, g + 1)
                    if not last:
                        turn_x(s + 1)
                    outputs(s, NPAIR - 1)
                    if not last:
                        pe.wait_ge(xa_split, (s + 1) * KC + KC)
                        project_z(s + 1, 0)
                        project_qk(s + 1, 0)
                    out_projection(s)
                    if not last:
                        values(s + 1)
                        pe.wait_ge(wo_added, s * SUPER + SUPER)
                        pe.wait_ge(state_kept, s * NPAIR + NPAIR)

                pe.wait_ge(aw_split, 5)
                pe.wait_ge(att_cleared, ATT_CLEARS)
                turn_x(0)
                pe.wait_ge(xa_split, KC)
                project_z(0, 0)
                project_qk(0, 0)
                values(0)
                with pe.Fori(0, NSUP - 1) as s:
                    supertile(s, False)
                supertile(NSUP - 1, True)

            for r in range(2):
                route(r)
                turn(r, 0, 0)
                pe.wait_ge(long_made, r + 1)
                with pe.Fori(0, E - 1) as e:
                    expert(r, e, False)
                expert(r, E - 1, True)
                if r == 0:
                    attention()

        @block.scalar
        def _(act):
            def copy(o, i):
                return nc.scalar.activation(o, i, ACT.Copy)

            steps = Steps(act, act_steps)

            def deviation(n, tiles):
                act.wait_ge(var_made, n)
                nc.scalar.activation(rstd[:, tiles], rstd[:, tiles], ACT.Sqrt).then_inc(std_made, 1)

            def route(r):
                if r:
                    deviation(QUARTERS + 1, slice(0, TILES))
                for s in range(NSUP):
                    if r == 0 and s % 2 == 0:
                        for q in range(0 if s == 0 else s // 2 + 1, min(s // 2 + 2, QUARTERS)):
                            deviation(q + 1, slice(q * QT, q * QT + QT))
                    act.wait_ge(xn_turned, r * NSUP + s + 1)
                    for kc in range(KC):
                        copy(xnt[s % 2][:, kc, :], bank[6 * (s % 2) + kc][:]).then_inc(xnt_copied, 1)
                act.wait_ge(gap_made, (r + 1) * QUARTERS)
                nc.scalar.activation(weight2[:], weight2[:], ACT.Exp).then_inc(exp_made, 1)

            def split_fc(u, k):
                raw, hi = ((raw_fc, fc_hi), (raw_g, gw_hi))[k // 4]
                at = (slice(None), k % 4 // 2, slice(k % 2 * 512, k % 2 * 512 + 512))
                copy(hi[at], raw[at]).then_inc(fc_hi_made, 1)

            def split_attention(n):
                w = (wq, wk, wz, wv, wo)[n]
                act.wait_ge(aw_staged[n], 16)
                copy(w[0].rearrange("p a n -> p (a n)"), raw_w[n]).then_inc(aw_hi_made, 1)

            def turned(r, e, n):
                w, buf = GROUPS[n][1], n % 2
                act.wait_ge(xg_turned, (r * E + e) * NG + n + 1)
                for kc in range(KC):
                    copy(xt_hi[buf][:, kc, 0:w], bank[6 + kc][:, 0:w]).then_inc(xt_hi_made, 1)

            def expert(r, e, last):
                u = r * E + e

                def gate(unit):
                    w, b, j = GROUPS[unit // HJ][1], unit % 2, unit % HJ
                    act.wait_ge(up_done, u * UNITS + unit + 1)
                    nc.scalar.activation(g_sb[b][:, 0:w], bank[2 + b][:, 0:w], ACT.Identity,
                                         bias=bias_now[:, j:j + 1]).then_inc(g_copied, 1)

                def silu(unit):
                    n, j, b = unit // HJ, unit % HJ, unit % 2
                    w = GROUPS[n][1]
                    act.wait_ge(hg_made, u * UNITS + unit + 1)
                    nc.scalar.activation(hg[b][:, 0:w], hg[b][:, 0:w], ACT.Silu).then_inc(silu_made, 1)
                    act.wait_ge(silu_made, u * UNITS + unit + 1)
                    copy(s_hi[n % 2][:, j, 0:w], hg[b][:, 0:w]).then_inc(s_hi_made, 1)

                def units(lo, hi):
                    gate(lo)
                    for unit in range(lo, hi):
                        if unit + 1 < hi:
                            gate(unit + 1)
                        silu(unit)
                        if unit in (HJ // 2, HJ + HJ // 2):
                            turned(r, e, unit // HJ + 1)
                        if 1 <= unit < 5:
                            k = 2 * (unit - 1)
                            act.wait_ge(proj_staged, u * 16 + 16)
                            copy(pr_hi[:, k:k + 2, :], raw_proj[:, k:k + 2, :]).then_inc(proj_hi_made, 1)

                act.wait_ge(bias_set, u + 1)
                units(0, 2 * HJ)
                with act.If(has_last_group(act, e)):
                    units(2 * HJ, UNITS)
                with act.Else():
                    act.drain().then_inc(g_copied, HJ)
                    act.drain().then_inc(silu_made, HJ)
                    act.drain().then_inc(s_hi_made, HJ)
                if not last:
                    act.wait_ge(fc_staged, u * 32 + 64)
                    for k in range(8):
                        split_fc(u + 1, k)
                    turned(r, e + 1, 0)
                elif r == 0:
                    split_attention(0)
                    split_attention(1)

            def attention():
                act.wait_ge(y_done, E * Y_TILES)
                for n in range(2, 5):
                    split_attention(n)

                def deviation4(s):
                    act.wait_ge(var4_made, s + 1)
                    nc.scalar.activation(rstd_now, rstd_now, ACT.Sqrt).then_inc(std4_made, 1)

                def split_x(s):
                    act.wait_ge(xna_turned, s + 1)
                    for kc in range(KC):
                        copy(xa[0][:, kc, :], bank[kc][:]).then_inc(xa_hi_made, 1)

                def log_decay(s, g, first=False):
                    G = s * NPAIR + g
                    act.wait_ge(z_done, G + 1)
                    if not first:
                        act.wait_ge(qk_made, G)
                    gate = far[:, :, :, 0:HALF]
                    z = bank[2][:].rearrange("p (a h n) -> p a h n", h=2, n=HALF)
                    nc.scalar.activation(gate, z, ACT.Exp, scale=-1.0, bias=bias_gate[:, g:g + 1]).then_inc(z_used, 1)
                    act.wait_ge(z_used, G + 1)
                    nc.scalar.activation(gate, gate, ACT.Ln, bias=1.0).then_inc(log_made, 1)

                def decays(s, g):
                    G = s * NPAIR + g
                    act.wait_ge(log_summed, G + 1)
                    n, f = near[:, :, :, 0:HALF], far[:, :, :, 0:HALF]
                    nc.scalar.activation(n, f, ACT.Exp, scale=-1.0).then_inc(near_made, 1)
                    act.wait_ge(near_made, G + 1)
                    nc.scalar.activation(f, f, ACT.Exp).then_inc(far_made, 1)

                def turned_keys(s, g):
                    act.wait_ge(k_turned, s * NPAIR + g + 1)
                    copy(kdt.rearrange("p a n -> p (a n)"), bank[6][:]).then_inc(kdt_copied, 1)

                def split_o(s, g):
                    act.wait_ge(o_done, s * NPAIR + g + 1)
                    copy(ot[0][:, g, :], bank[5][:]).then_inc(ot_hi_made, 1)

                def values(s):
                    for n in range(2 * SUPER):
                        act.wait_ge(v_done, s * 8 + n + 1)
                        copy(v_sb[:, n // 2, n % 2 * 512:n % 2 * 512 + 512], bank[5 + n % 2][:]).then_inc(v_copied, 1)

                def supertile(s, last):
                    for g in range(NPAIR):
                        if g + 1 < NPAIR:
                            log_decay(s, g + 1)
                        turned_keys(s, g)
                        if g + 1 < NPAIR:
                            decays(s, g + 1)
                        if g:
                            split_o(s, g - 1)
                        if g == SUPER + 1 and not last:
                            deviation4(s + 1)
                    if not last:
                        split_x(s + 1)
                    split_o(s, NPAIR - 1)
                    if not last:
                        log_decay(s + 1, 0)
                        decays(s + 1, 0)
                        values(s + 1)

                deviation4(0)
                split_x(0)
                log_decay(0, 0, first=True)
                decays(0, 0)
                values(0)
                with act.Fori(0, NSUP - 1) as s:
                    supertile(s, False)
                supertile(NSUP - 1, True)

            for r in range(2):
                route(r)
                act.wait_ge(fc_staged, r * E * 32 + 32)
                for k in range(8):
                    split_fc(r * E, k)
                turned(r, 0, 0)
                act.wait_ge(long_made, r + 1)
                with act.Fori(0, E - 1) as e:
                    expert(r, e, False)
                expert(r, E - 1, True)
                if r == 0:
                    attention()

        @block.vector
        def _(dve):
            steps = Steps(dve, dve_steps)
            v = nc.vector

            v.memset(as_f32(halves[:, 0:CLEAR_ROWS * C]), 0.0).then_inc(zero_made, 1)
            dve.wait_ge(small_loaded, 16 * 5)
            dve.wait_ge(consts_made, CONSTS)
            for n, o in enumerate((bias_fc, bias_g, bias_gate)):
                dve.wait_ge(bias_turned, n + 1)
                steps.after(v.tensor_scalar(o[:], bank[n][:, 0:o.shape[1]], -1.0 if o is bias_gate else 1.0, None,
                                            ALU.mult))

            def tile_of(t, i):
                return t[:, bass.ds(i, 1), :].rearrange("p a c -> p (a c)")

            def tile_stats(i):
                return v.bn_stats(tile_of(stats, i), tile_of(x, i))

            def variance(halves_of, mean, var, out_):
                mean1, sq1, mean2, sq2 = (halves_of[:, :, n] for n in (1, 2, 4, 5))
                steps.after(v.tensor_tensor(out_, mean1, mean2, ALU.subtract))
                steps.after(v.tensor_tensor(out_, out_, out_, ALU.mult))
                steps.after(v.tensor_tensor(var, sq1, sq2, ALU.add))
                steps.after(v.tensor_scalar(var, var, 1.0 / C, EPS, ALU.mult, ALU.add))
                steps.after(v.tensor_tensor(mean, mean1, mean2, ALU.add))
                steps.after(v.tensor_scalar(mean, mean, 0.5, None, ALU.mult))
                return v.scalar_tensor_tensor(out_, out_, 0.25, var, ALU.mult, ALU.add)

            def inverse_deviation(n, tiles):
                of = stats[:, tiles, :]
                variance(of, of[:, :, 1], of[:, :, 2], rstd[:, tiles]).then_inc(var_made, 1)
                dve.wait_ge(std_made, n)
                steps.after(v.reciprocal(rstd[:, tiles], rstd[:, tiles]))

            def choose(of, k, q):
                tiles = slice(q * QT, q * QT + QT)
                wide_ = [P, QT, E]
                ranks = rank[:].unsqueeze(1).to_broadcast(wide_)
                t, found = top[k], best[:, k * TILES + q * QT:k * TILES + q * QT + QT]
                steps.after(v.tensor_reduce(t, of, AX_X, ALU.max))
                steps.after(v.tensor_tensor(chosen, of, t.unsqueeze(2).to_broadcast(wide_), ALU.is_equal))
                steps.after(v.tensor_tensor(chosen, chosen, ranks, ALU.mult))
                steps.after(v.tensor_reduce(found, chosen, AX_X, ALU.max))
                steps.after(v.tensor_tensor(chosen, ranks, found.unsqueeze(2).to_broadcast(wide_), ALU.is_equal))
                if k == 0:
                    picks = hot[:, q * QT * E:(q + 1) * QT * E].rearrange("p (e j) -> p j e", e=E)
                else:
                    picks = hot[:, TILES * E:PICKS * E].rearrange("p (e j) -> p j e", e=E)[:, tiles, :]
                v.tensor_copy(picks, chosen).then_inc(hot_made[k], 1)

            def choices(r, q):
                tiles = slice(q * QT, q * QT + QT)
                of = logits
                dve.wait_ge(logits_done, r * NSUP + 2 * q + 2)
                steps.after(v.tensor_tensor(of, bank[(2, 5)[q % 2]][:, q * QT * E:(q + 1) * QT * E].rearrange("p (i e) -> p i e", e=E),
                                            router_bias[:].unsqueeze(1).to_broadcast([P, QT, E]), ALU.add))
                choose(of, 0, q)
                dve.wait_ge(hot_made[0], r * QUARTERS + q + 1)
                steps.after(v.scalar_tensor_tensor(of, chosen, -BIG, of, ALU.mult, ALU.add))
                choose(of, 1, q)
                v.tensor_tensor(weight2[:, tiles], top[1], top[0], ALU.subtract).then_inc(gap_made, 1)
                dve.wait_ge(gap_made, r * QUARTERS + q + 1)

            def set_resume(tiles):
                t = resume[:, 0:tiles * E]
                steps.after(v.memset(t, 1.0))
                steps.after(v.memset(t.rearrange("p (e j) -> p e j", e=E)[:, :, 0:1], 0.0))

            def give_slots(r, n):
                k, first, tiles = BLOCKS[n]
                picks = slice(k * TILES + first, k * TILES + first + tiles)
                cols = slice(picks.start * E, picks.stop * E)
                t = taken[:, 0:tiles * E]
                by_expert = t.rearrange("p (e j) -> p e j", e=E)
                psum = [bank[i][:, cols].rearrange("p (e j) -> p e j", e=E) for i in (3, 4)]
                ov, fs, at = over[:, 0:tiles], first_slot[:, 0:tiles], pos[:, picks]
                dve.wait_ge(counted, r * len(BLOCKS) + n + 1)
                steps.after(v.tensor_tensor_scan(t, resume[:, 0:tiles * E], bank[4][:, cols], 0.0, ALU.mult, ALU.add))
                earlier, now = given[n % 2], given[(n + 1) % 2]
                steps.after(v.tensor_tensor(now, earlier, by_expert[:, :, tiles - 1], ALU.add))
                steps.after(v.tensor_tensor(by_expert, by_expert, psum[1], ALU.subtract))
                steps.after(v.tensor_tensor(by_expert, by_expert, psum[0], ALU.add))
                steps.after(v.tensor_tensor(by_expert, by_expert, earlier.unsqueeze(2).to_broadcast([P, E, tiles]),
                                            ALU.add))
                steps.after(v.tensor_tensor(t, t, hot[:, cols], ALU.mult))
                steps.after(v.tensor_reduce(at, t.rearrange("p (e j) -> p j e", e=E), AX_X, ALU.add))
                steps.after(v.tensor_scalar(fs, best[:, picks], -float(CAP), float(E * CAP), ALU.mult, ALU.add))
                steps.after(v.tensor_scalar(ov, at, float(CAP), float(SKIP), ALU.is_ge, ALU.mult))
                steps.after(v.tensor_tensor(ov, ov, fs, ALU.add))
                v.tensor_tensor(write_slot[:, picks], ov, at, ALU.add).then_inc(slots_made, 1)
                dve.wait_ge(slots_made, r * len(BLOCKS) + n + 1)
                steps.after(v.tensor_scalar(ov, at, float(CAP - 1), None, ALU.min))
                steps.after(v.tensor_tensor(read_slot[:, picks], ov, fs, ALU.add))

            def route(r):
                def rows_of(q):
                    if r == 0:
                        dve.wait_ge(x_loaded[q], 16)
                        for t in range(q * QT, (q + 1) * QT):
                            v.bn_stats(stats[:, t, :], x[:, t, :]).then_inc(stats_made, 1)
                        dve.wait_ge(stats_made, (q + 1) * QT)
                        inverse_deviation(q + 1, slice(q * QT, (q + 1) * QT))
                    elif q == 0:
                        dve.wait_ge(stats_made, 2 * TILES)
                        inverse_deviation(QUARTERS + 1, slice(0, TILES))
                    for i in range(q * QT, (q + 1) * QT):
                        v.tensor_scalar(xn[:, i, :], x[:, i, :], stats[:, i, 1:2], rstd[:, i:i + 1],
                                        ALU.subtract, ALU.mult).then_inc(xn_made, 1)

                rows_of(0)
                steps.after(v.memset(ones, 1.0))
                steps.after(v.memset(given[0], 0.0))
                set_resume(QT)
                rows_of(1)
                for q in range(QUARTERS):
                    if q + 2 < QUARTERS:
                        rows_of(q + 2)
                    choices(r, q)
                    give_slots(r, q)
                set_resume(TILES)
                give_slots(r, QUARTERS)
                v.tensor_scalar(long[:], given[(QUARTERS + 1) % 2][0:1, :], float(GROUPS[-1][0]), None,
                                ALU.is_gt).then_inc(long_made, 1)
                dve.wait_ge(long_made, r + 1)
                dve.wait_ge(exp_made, r + 1)
                steps.after(v.tensor_scalar(weight1[:], weight2[:], 1.0, None, ALU.add))
                steps.after(v.reciprocal(weight1[:], weight1[:]))
                steps.after(v.scalar_tensor_tensor(weight2[:], weight2[:], 0.5, weight1[:], ALU.mult, ALU.mult))
                steps.after(v.tensor_scalar(weight1[:], weight1[:], 0.5, None, ALU.mult))

            def split_fc(done, k):
                raw, hi, lo = ((raw_fc, fc_hi, fc_lo), (raw_g, gw_hi, gw_lo))[k // 4]
                at = (slice(None), k % 4 // 2, slice(k % 2 * 512, k % 2 * 512 + 512))
                dve.wait_ge(fc_hi_made, done + k + 1)
                v.tensor_tensor(lo[at], raw[at], as_f32(hi[at]), ALU.subtract).then_inc(fc_split, 1)

            def split_attention(n):
                w = (wq, wk, wz, wv, wo)[n]
                dve.wait_ge(aw_hi_made, n + 1)
                v.tensor_tensor(w[1].rearrange("p a n -> p (a n)"), raw_w[n],
                                as_f32(w[0].rearrange("p a n -> p (a n)")), ALU.subtract).then_inc(aw_split, 1)

            def turned(r, e, n):
                w, buf = GROUPS[n][1], n % 2
                for kc in range(KC):
                    dve.wait_ge(xt_hi_made, ((r * E + e) * NG + n) * KC + kc + 1)
                    i = v.tensor_tensor(xt_lo[buf][:, kc, 0:w], bank[6 + kc][:, 0:w],
                                        as_f32(xt_hi[buf][:, kc, 0:w]), ALU.subtract)
                i.then_inc(xt_split, 1)

            def expert(r, e, last):
                u = r * E + e

                def product(unit):
                    w, b, col = GROUPS[unit // HJ][1], unit % 2, e * HJ + unit % HJ
                    dve.wait_ge(g_copied, u * UNITS + unit + 1)
                    if unit != 1:
                        dve.wait_ge(s_split, u * UNITS + max(unit - 1, 0))
                    v.scalar_tensor_tensor(hg[b][:, 0:w], bank[b][:, 0:w], bias_fc[:, bass.ds(col, 1)],
                                           g_sb[b][:, 0:w], ALU.add, ALU.mult).then_inc(hg_made, 1)

                def low(unit):
                    n, j, b = unit // HJ, unit % HJ, unit % 2
                    w, buf = GROUPS[n][1], n % 2
                    dve.wait_ge(s_hi_made, u * UNITS + unit + 1)
                    v.tensor_tensor(s_lo[buf][:, j, 0:w], hg[b][:, 0:w], as_f32(s_hi[buf][:, j, 0:w]),
                                    ALU.subtract).then_inc(s_split, 1)

                def project_low(k):
                    dve.wait_ge(proj_hi_made, u * 4 + k + 1)
                    at = (slice(None), slice(2 * k, 2 * k + 2), slice(None))
                    v.tensor_tensor(pr_lo[at], raw_proj[at], as_f32(pr_hi[at]), ALU.subtract).then_inc(proj_split, 1)

                def y_out(t):
                    n = t // 4 if t < 8 else 2
                    m = GROUP_TILES[n][t - 4 * n][1]
                    dve.wait_ge(y_done, u * Y_TILES + t + 1)
                    dve.wait_ge(y_stored[t % 2], (u * (Y_TILES // 2) + t // 2) * 16)
                    v.tensor_tensor(y_sb[0:m, t % 2, :], bank[4 + t % 2][0:m, 0:C], y_bias[0:m, :],
                                    ALU.add).then_inc(y_copied, 1)

                v.tensor_scalar(bias_now[:], bias_g[:, bass.ds(e * HJ, HJ)], 1.0, None, ALU.mult
                                ).then_inc(bias_set, 1)
                dve.wait_ge(bias_loaded, u * 16 + 16)
                for unit in range(2 * HJ):
                    product(unit)
                    if unit:
                        low(unit - 1)
                    if unit in (HJ // 2 + 1, HJ + HJ // 2 + 1):
                        turned(r, e, unit // HJ + 1)
                    if 2 <= unit < 6:
                        project_low(unit - 2)
                low(2 * HJ - 1)
                for t in range(4):
                    y_out(t)
                with dve.If(has_last_group(dve, e)):
                    for unit in range(2 * HJ, UNITS):
                        product(unit)
                        if unit > 2 * HJ:
                            low(unit - 1)
                    low(UNITS - 1)
                with dve.Else():
                    dve.drain().then_inc(hg_made, HJ)
                    dve.drain().then_inc(s_split, HJ)
                for t in range(4, Y_TILES):
                    if not last and t < 8:
                        split_fc(u * 8 + 8, 2 * (t - 4))
                        split_fc(u * 8 + 8, 2 * (t - 4) + 1)
                    if not last and t == 8:
                        turned(r, e + 1, 0)
                    if last and r == 0 and t in (6, 8):
                        split_attention((t - 6) // 2)
                    y_out(t)

            def add_rows(r, i, got_rows):
                for k, w in enumerate((weight1, weight2)):
                    ins = v.scalar_tensor_tensor(tile_of(x, i), got_rows[:, k, :], w[:, bass.ds(i, 1)],
                                                 tile_of(x, i), ALU.mult, ALU.add)
                    if k == 0:
                        ins.then_inc(row1_added, 1)
                        dve.wait_ge(row1_added, r * TILES + i + 1)
                    else:
                        ins.then_inc(combined, 1)

            def combine_last():
                with dve.Fori(0, TILES // RING) as o:
                    for b in range(RING):
                        before = TILES // SUPER if b < SUPER else 0
                        dve.wait_ge(rows_got[b], (before + o + 1) * TOPK * 16)
                        add_rows(1, o * RING + b, got[:, b, :, :])

            def attention():
                for n in range(2, 5):
                    split_attention(n)
                dve.wait_ge(aw_split, 5)
                v.memset(state, 0.0).then_inc(att_cleared, 1)
                for t in (near, far):
                    v.memset(t[:, :, 0, HALF:HALF + 1], 1.0).then_inc(att_cleared, 1)
                for h in range(2):
                    v.memset(prob[h][HALF:P, :, 0:HALF], 0.0).then_inc(att_cleared, 1)
                dve.wait_ge(att_cleared, ATT_CLEARS)
                lower, upper = slice(0, HALF), slice(HALF, P)

                def combine(s, b):
                    dve.wait_ge(rows_got[b], (s + 1) * TOPK * 16)
                    add_rows(0, s * SUPER + b, got4[:, b, :, :])

                def statistics(s):
                    for b in range(SUPER):
                        i = s * SUPER + b
                        dve.wait_ge(combined, i + 1)
                        dve.sem_inc(x_settled, 1)
                        v.bn_stats(stats_now[:, b, :], tile_of(x, i)).then_inc(stats4_made, 1)
                    dve.wait_ge(stats4_made, s * SUPER + SUPER)
                    variance(stats_now, mean_now, var_now, rstd_now).then_inc(var4_made, 1)

                def normalise(s):
                    dve.wait_ge(std4_made, s + 1)
                    steps.after(v.reciprocal(rstd_now, rstd_now))
                    for b in range(SUPER):
                        v.tensor_scalar(xna[:, b, :], tile_of(x, s * SUPER + b), mean_now[:, b:b + 1],
                                        rstd_now[:, b:b + 1], ALU.subtract, ALU.mult).then_inc(xna_made, 1)

                def split_x(s):
                    for kc in range(KC):
                        dve.wait_ge(xa_hi_made, s * KC + kc + 1)
                        v.tensor_tensor(xa[1][:, kc, :], bank[kc][:], as_f32(xa[0][:, kc, :]),
                                        ALU.subtract).then_inc(xa_split, 1)

                def sum_logs(s, g):
                    dve.wait_ge(log_made, s * NPAIR + g + 1)
                    for c in range(SUPER):
                        for gates in (far[:, c, 0, HALF - 1::-1], far[:, c, 1, 0:HALF]):
                            ins = v.tensor_tensor_scan(gates, gates, limit[:], 0.0, ALU.add, ALU.min)
                    ins.then_inc(log_summed, 1)

                def scaled(s, g):
                    G = s * NPAIR + g
                    dve.wait_ge(far_made, G + 1)
                    v.tensor_copy(carry[:, g % 2, 0:1], near[:, 0, 0, 0:1])
                    v.tensor_tensor(carry[:, g % 2, 1:SUPER], near[:, 1:SUPER, 0, 0], near[:, 0:SUPER - 1, 1, HALF - 1],
                                    ALU.mult)
                    v.tensor_copy(leave[:, g % 2:g % 2 + 1], near[:, SUPER - 1, 1, HALF - 1:HALF])
                    dve.wait_ge(qk_done, G + 1)
                    bq, bk = (bank[n][:].rearrange("p (a n) -> p a n", n=P) for n in (0, 1))
                    first, second = (slice(None), slice(None), 0, slice(1, HALF + 1)), (slice(None), slice(None), 1, lower)
                    q = qd[g % 2]
                    for o, i, w, part_, at in ((q, bq, far, lower, first), (q, bq, near, upper, second),
                                               (kd, bk, near, lower, first), (kd, bk, far, upper, second)):
                        ins = v.tensor_tensor(o[:, :, part_], i[:, :, part_], w[at], ALU.mult)
                    ins.then_inc(qk_made, 1)

                def mask(s, g):
                    G = s * NPAIR + g
                    dve.wait_ge(scores_done, G + 1)
                    if g:
                        dve.wait_ge(o_done, G)
                    for h in range(2):
                        sc = bank[3 + h][:].rearrange("p (a n) -> p a n", n=P)
                        v.tensor_tensor(prob[h][lower, :, :], sc[lower, :, :],
                                        causal[lower, :].unsqueeze(1).to_broadcast([HALF, SUPER, P]), ALU.mult)
                        ins = v.tensor_tensor(prob[h][upper, :, upper], sc[upper, :, upper],
                                              causal[upper, upper].unsqueeze(1).to_broadcast([HALF, SUPER, HALF]),
                                              ALU.mult)
                    ins.then_inc(prob_made, 1)

                def chain(s, g):
                    G = s * NPAIR + g
                    dve.wait_ge(qk_made, G + 1)
                    dve.wait_ge(kv_done, G + 1)
                    for c in range(SUPER):
                        src = state[:, g, :] if c == 0 else state_sum[:]
                        two = "p (h n) -> p h n"
                        v.scalar_tensor_tensor(state_in[:, c, :].rearrange(two, h=2), src.rearrange(two, h=2),
                                               carry[:, g % 2, c:c + 1],
                                               head_of[:].unsqueeze(2).to_broadcast([P, 2, DH]),
                                               ALU.mult, ALU.mult).then_inc(state_ready, 1)
                        dve.wait_ge(state_ready, G * SUPER + c + 1)
                        steps.after(v.tensor_tensor(state_sum[:], bank[7][:, c * P:(c + 1) * P],
                                                    state_in[:, c, :], ALU.add))
                    v.tensor_scalar(state[:, g, :], state_sum[:], leave[:, g % 2:g % 2 + 1], None,
                                    ALU.mult).then_inc(state_kept, 1)
                    dve.wait_ge(state_kept, G + 1)

                def split_o(s, g):
                    dve.wait_ge(ot_hi_made, s * NPAIR + g + 1)
                    v.tensor_tensor(ot[1][:, g, :], bank[5][:], as_f32(ot[0][:, g, :]),
                                    ALU.subtract).then_inc(ot_split, 1)

                def add_output(s, b):
                    i = s * SUPER + b
                    dve.wait_ge(wo_done, i + 1)
                    v.tensor_tensor(tile_of(x, i), bank[3 + b % 2][:, 0:C], tile_of(x, i),
                                    ALU.add).then_inc(wo_added, 1)

                def supertile(s, last):
                    for g in range(NPAIR):
                        if g:
                            chain(s, g - 1)
                        if g + 1 < NPAIR:
                            sum_logs(s, g + 1)
                        if not last:
                            if 1 <= g <= SUPER:
                                combine(s + 1, g - 1)
                            elif g == SUPER + 1:
                                statistics(s + 1)
                            elif g == SUPER + 2:
                                normalise(s + 1)
                        mask(s, g)
                        if g:
                            split_o(s, g - 1)
                        if g + 1 < NPAIR:
                            scaled(s, g + 1)
                    chain(s, NPAIR - 1)
                    if not last:
                        split_x(s + 1)
                    split_o(s, NPAIR - 1)
                    if not last:
                        sum_logs(s + 1, 0)
                    add_output(s, 0)
                    add_output(s, 1)
                    if not last:
                        scaled(s + 1, 0)
                    add_output(s, 2)
                    add_output(s, 3)
                    for b in range(SUPER):
                        i = s * SUPER + b
                        dve.wait_ge(wo_added, i + 1)
                        dve.sem_inc(x_settled, 1)
                        tile_stats(i).then_inc(stats_made, 1)

                for b in range(SUPER):
                    combine(0, b)
                statistics(0)
                normalise(0)
                split_x(0)
                sum_logs(0, 0)
                scaled(0, 0)
                steps.loop(0, NSUP - 1, NPAIR * SUPER + 7, lambda s: supertile(s, False))
                supertile(NSUP - 1, True)

            for r in range(2):
                route(r)
                for k in range(8):
                    split_fc(r * E * 8, k)
                turned(r, 0, 0)
                with dve.Fori(0, E - 1) as e:
                    expert(r, e, False)
                expert(r, E - 1, True)
                if r == 0:
                    attention()
            combine_last()


_INS = ["L0_attn_x", "L0_attn_W_q", "L0_attn_W_k", "L0_attn_W_v", "L0_attn_W_gate", "L0_attn_b_gate",
        "L0_attn_W_o", "L0_ffn_router_w", "L0_ffn_router_b", "L0_ffn_w_c_fc", "L0_ffn_b_c_fc",
        "L0_ffn_w_gate", "L0_ffn_b_gate", "L0_ffn_w_c_proj", "L0_ffn_b_c_proj"]


def kernel(**inputs):
    import numpy as _np
    import concourse.bacc as _bacc
    from concourse.bass_utils import run_bass_kernel_spmd as _run

    nc = _bacc.Bacc("TRN2", target_bir_lowering=False, num_devices=1)
    arrays, args = {}, []
    for name in _INS:
        a = _np.ascontiguousarray(inputs[name])
        arrays[f"in_{name}"] = a
        args.append(nc.dram_tensor(f"in_{name}", a.shape, mybir.dt.from_np(a.dtype), kind="ExternalInput").ap())
    args.append(nc.dram_tensor("out_x", (1, T, C), F32, kind="ExternalOutput").ap())
    macaron(nc, *args)
    r = _run(nc, [arrays], core_ids=[0])
    return r.results[0]["out_x"]
```

```python
from contextlib import ExitStack

import concourse.bass as bass
from concourse import mybir

ALU = mybir.AluOpType
ACT = mybir.ActivationFunctionType
AX_X = mybir.AxisListType.X
F32 = mybir.dt.float32
F32R = mybir.dt.float32r
BF16 = mybir.dt.bfloat16
U32 = mybir.dt.uint32

P = 128
T = 4096
C = 256
KC = C // P
TILES = T // P
EPS = 1e-5

E = 8
TOPK = 2
HID = 1024
HJ = HID // P
CAP = int(1.2 * TOPK * T // E)
ROWS = E * CAP
PICKS = TOPK * TILES
SKIP = 1 << 17
BIG = 1e30
GROUPS = [(s, min(512, CAP - s)) for s in range(0, CAP, 512)]
GROUP_TILES = [[(o, min(P, n - o)) for o in range(0, n, P)] for _, n in GROUPS]
NARROW = 384
Y_TILES = sum(len(t) for t in GROUP_TILES)
NG = len(GROUPS)
UNITS = NG * HJ

HEADS = 16
DH = 64
NPAIR = HEADS * DH // P
SUPER = 4
NSUP = TILES // SUPER
QUARTERS = 4
QT = TILES // QUARTERS
SW = SUPER * P
HALF = P // 2
LIMIT = 80.0

BLOCKS = [(0, q * QT, QT) for q in range(QUARTERS)] + [(1, 0, TILES)]

CLEAR_ROWS = 8
CLEAR = CLEAR_ROWS * P
CLEARS = -(-ROWS // CLEAR)
CONSTS = 5
ATT_CLEARS = 8
assert ROWS % CLEAR_ROWS == 0 and NG == 3 and Y_TILES % 2 == 0


class Steps:

    def __init__(self, eng, sem):
        self.eng, self.sem, self.base, self.n = eng, sem, 0, 0

    def after(self, ins):
        ins.then_inc(self.sem, 1)
        self.n += 1
        self.eng.wait_ge(self.sem, self.base + self.n)

    def loop(self, lo, hi, per, body):
        start = self.base + self.n
        with self.eng.Fori(lo, hi) as i:
            self.base, self.n = start + (i - lo) * per, 0
            body(i)
            assert self.n == per, (self.n, per)
        self.base, self.n = start + (hi - lo) * per, 0


def macaron(nc, x_in, w_q, w_k, w_v, w_gate, b_gate, w_o, router_w, router_b,
            w_fc, b_fc, w_g, b_g, w_proj, b_proj, out):
    with ExitStack() as ctx:
        def sb(name, shape, dt=F32):
            return ctx.enter_context(nc.sbuf_tensor(name, shape, dt))

        def sem(name):
            return ctx.enter_context(nc.semaphore(name))

        expert_in = nc.dram_tensor("expert_in", (ROWS, C), F32, kind="Internal").ap()
        expert_out = nc.dram_tensor("expert_out", (ROWS, C), F32, kind="Internal").ap()

        x = sb("x", [P, TILES, C])
        wide = sb("wide", [P, 8192])
        temp = sb("temp", [P, 2048])
        rows = sb("rows", [P, 1024])
        halves = sb("halves", [P, 32768], F32R)
        ident = sb("ident", [P, P])
        causal = sb("causal", [P, P], BF16)
        before = sb("before", [P, P], BF16)
        limit = sb("limit", [P, HALF], BF16)
        rank = sb("rank", [P, E])
        router = sb("router", [P, KC, E])
        router_bias = sb("router_bias", [P, E])
        rstd = sb("rstd", [P, TILES])
        read_slot = sb("read_slot", [P, PICKS], U32)
        weight1 = sb("weight1", [P, TILES])
        weight2 = sb("weight2", [P, TILES])
        bias_fc = sb("bias_fc", [P, E * HJ])
        bias_g = sb("bias_g", [P, E * HJ])
        bias_gate = sb("bias_gate", [P, NPAIR])
        stats = sb("stats", [P, TILES, 6])
        bias_now = sb("bias_now", [P, HJ])
        carry = sb("carry", [P, 2, SUPER + 2])
        spare = sb("spare", [P, P])
        long = sb("long", [1, 2 * E], U32)

        def part(t, at, *dims):
            n = 1
            for d in dims:
                n *= d
            v = t[:, at:at + n]
            names = "abc"[:len(dims)]
            if len(dims) == 1:
                return v
            return v.rearrange(f"p ({' '.join(names)}) -> p {' '.join(names)}",
                               **{names[i]: dims[i] for i in range(1, len(dims))})

        xn = part(wide, 0, TILES, C)
        raw_fc = part(wide, 0, KC, HID)
        raw_g = part(wide, 2048, KC, HID)
        raw_proj = part(wide, 4096, HJ, C)
        xg = [part(wide, 6144, 4, C), part(wide, 7168, 4, C)]
        got = [part(wide, 0, TILES, C), part(halves, 0, TILES, C).bitcast(F32)]
        g_sb = [part(temp, 0, 512), part(temp, 512, 512)]
        hg = [part(temp, 1024, 512), part(temp, 1536, 512)]
        y_sb = part(rows, 0, 2, C)
        y_bias = part(rows, 512, C)
        fc_hi, fc_lo, gw_hi, gw_lo = (part(halves, 2048 * i, KC, HID) for i in range(4))
        pr_hi, pr_lo = (part(halves, 2048 * i, HJ, C) for i in (4, 5))
        s_hi = [part(halves, 12288 + 8192 * i, HJ, 512) for i in range(2)]
        s_lo = [part(halves, 16384 + 8192 * i, HJ, 512) for i in range(2)]
        xt_hi = [part(halves, 28672 + 2048 * i, KC, 512) for i in range(2)]
        xt_lo = [part(halves, 29696 + 2048 * i, KC, 512) for i in range(2)]
        xnt = [part(rows, 0, KC, SW), part(temp, 0, KC, SW)]
        taken = part(temp, 1024, 256)
        hot = part(temp, 1280, 256).bitcast(BF16)
        resume = part(temp, 1536, 128).bitcast(BF16)
        logits = part(temp, 1664, QT, E)
        chosen = part(temp, 1728, QT, E)
        pos = part(temp, 1792, PICKS)
        best = part(temp, 1856, PICKS)
        write_slot = part(temp, 1920, PICKS).bitcast(U32)
        top = [part(temp, 1984, QT), part(temp, 1992, QT)]
        given = [part(temp, 2000, E), part(temp, 2008, E)]
        first_slot = part(temp, 2016, TILES)
        ones = part(spare, 0, P // 2).bitcast(BF16)
        over = part(spare, P // 2, TILES)
        reads = [weight1[:], part(spare, P // 2 + TILES, TILES)]
        v_sb = part(wide, 0, SUPER, HEADS * DH)
        near = part(wide, 4096, SUPER, 2 * (HALF + 1)).rearrange("p a (h n) -> p a h n", h=2)
        far = part(wide, 4616, SUPER, 2 * (HALF + 1)).rearrange("p a (h n) -> p a h n", h=2)
        qd = [part(wide, 5136, SUPER, P), part(wide, 5648, SUPER, P)]
        kd = part(wide, 6160, SUPER, P)
        prob = [part(wide, 6672, SUPER, P), part(wide, 7184, SUPER, P)]
        stats_now = part(wide, 7696, SUPER, 6)
        mean_now, var_now, rstd_now, step_now = (part(wide, 7720 + SUPER * i, SUPER) for i in range(4))
        kdt = part(temp, 0, SUPER, P)
        state_in = part(temp, 512, SUPER, P)
        state = part(temp, 1024, NPAIR, DH)
        factors = part(temp, 1536, DH * (SUPER + 2))
        states = part(wide, 7736, DH * (SUPER + 2))
        xna = part(rows, 0, SUPER, C)
        raw_w = [part(wide, 2048 * i, 2048) for i in range(4)] + [part(temp, 0, 2048)]
        wq, wk, wz, wv = ([part(halves, 4096 * i, KC, 1024), part(halves, 4096 * i + 2048, KC, 1024)]
                          for i in range(4))
        wo = [part(halves, 16384, NPAIR, C), part(halves, 18432, NPAIR, C)]
        xa = [part(halves, 20480, KC, SW), part(halves, 21504, KC, SW)]
        ot = [part(halves, 22528, NPAIR, SW), part(halves, 26624, NPAIR, SW)]
        got4 = part(halves, 30720, SUPER, TOPK, C).bitcast(F32)

        bank = [ctx.enter_context(nc.psum_tensor(f"bank{i}", [P, 512], F32)) for i in range(8)]

        x_loaded = [sem(f"x_loaded{i}") for i in range(4)]
        small_loaded = sem("small_loaded")
        consts_made = sem("consts_made")
        pool_steps = sem("pool_steps")
        zero_made = sem("zero_made")
        cleared = sem("cleared")
        bias_turned, bias_set, biases_used = sem("bias_turned"), sem("bias_set"), sem("biases_used")
        stats_made, x_settled = sem("stats_made"), sem("x_settled")
        dve_steps = sem("dve_steps")
        var_made = sem("var_made")
        std_made = sem("std_made")
        xn_made = sem("xn_made")
        xn_turned = sem("xn_turned")
        xnt_copied = sem("xnt_copied")
        logits_done = sem("logits_done")
        gap_made = sem("gap_made")
        exp_made = sem("exp_made")
        hot_made = [sem("hot_made0"), sem("hot_made1")]
        counted, long_made = sem("counted"), sem("long_made")
        slots_made = sem("slots_made")
        scattered = [sem(f"scattered{i}") for i in range(4)]
        fc_staged = sem("fc_staged")
        proj_staged = sem("proj_staged")
        fc_hi_made, fc_split = sem("fc_hi_made"), sem("fc_split")
        proj_hi_made, proj_split = sem("proj_hi_made"), sem("proj_split")
        bias_loaded = sem("bias_loaded")
        xg_loaded = [sem("xg_loaded0"), sem("xg_loaded1")]
        xg_turned = sem("xg_turned")
        xt_hi_made, xt_split = sem("xt_hi_made"), sem("xt_split")
        up_done = sem("up_done")
        g_copied = sem("g_copied")
        hg_made = sem("hg_made")
        silu_made = sem("silu_made")
        s_hi_made, s_split = sem("s_hi_made"), sem("s_split")
        y_done = sem("y_done")
        y_copied = sem("y_copied")
        y_stored = [sem("y_stored0"), sem("y_stored1")]
        rows_got = [sem(f"rows_got{i}") for i in range(TILES)]
        earlier_got = sem("earlier_got")
        row1_added, combined = sem("row1_added"), sem("combined")
        aw_staged = [sem(f"aw_staged{i}") for i in range(5)]
        aw_hi_made, aw_split = sem("aw_hi_made"), sem("aw_split")
        stats4_made, var4_made = sem("stats4_made"), sem("var4_made")
        log_var4_made, rstd4_made = sem("log_var4_made"), sem("rstd4_made")
        att_cleared = sem("att_cleared")
        xna_made, xna_turned = sem("xna_made"), sem("xna_turned")
        xa_hi_made, xa_split = sem("xa_hi_made"), sem("xa_split")
        z_done, q_done, k_done = sem("z_done"), sem("q_done"), sem("k_done")
        z_used, log_made, log_summed = sem("z_used"), sem("log_made"), sem("log_summed")
        near_made, far_made, qk_made = sem("near_made"), sem("far_made"), sem("qk_made")
        v_done, v_copied = sem("v_done"), sem("v_copied")
        k_turned, kdt_copied = sem("k_turned"), sem("kdt_copied")
        scores_done, prob_made = sem("scores_done"), sem("prob_made")
        kv_done, state_ready, state_kept = sem("kv_done"), sem("state_ready"), sem("state_kept")
        o_done, ot_hi_made, ot_split = sem("o_done"), sem("ot_hi_made"), sem("ot_split")
        wo_done, wo_added = sem("wo_done"), sem("wo_added")
        stored = sem("stored")

        block = ctx.enter_context(nc.Block())

        def wait_past(eng, sem_, value):
            if not (isinstance(value, int) and value == 0):
                eng.wait_ge(sem_, value)

        def as_f32(ap):
            return ap.bitcast(F32)

        def has_last_group(eng, e):
            return eng.value_load(long[0:1, bass.ds(e, 1)], min_val=0, max_val=1)

        def fills_group1(eng, e):
            return eng.value_load(long[0:1, bass.ds(E + e, 1)], min_val=0, max_val=1)

        def passes(hi_lo_a, hi_lo_b):
            (ah, al), (bh, bl) = hi_lo_a, hi_lo_b
            return [(ah, bh), (ah, bl), (al, bh)]

        tok = "(i p) c -> p i c"

        @block.sync
        def _(sp):
            sp.dma_start(router[:], router_w.rearrange("(a p) e -> p a e", p=P)).then_inc(small_loaded, 16)
            sp.dma_start(router_bias[:], router_b.rearrange("(a e) -> a e", a=1).to_broadcast([P, E])).then_inc(small_loaded, 16)
            sp.dma_start(rows[0:E * HJ, 0:P], b_fc.rearrange("e a (j p) -> (e a j) p", p=P)).then_inc(small_loaded, 16)
            sp.dma_start(rows[0:E * HJ, P:2 * P], b_g.rearrange("e a (j p) -> (e a j) p", p=P)).then_inc(small_loaded, 16)
            sp.dma_start(rows[0:NPAIR, 2 * P:3 * P], b_gate.rearrange("(j p) -> j p", p=P)).then_inc(small_loaded, 16)
            for b in range(2):
                sp.sem_inc(y_stored[b], 16)
            for i in range(4):
                n = TILES // 4
                sp.dma_start(x[:, i * n:(i + 1) * n, :],
                             x_in[0, i * n * P:(i + 1) * n * P, :].rearrange(tok, p=P)).then_inc(x_loaded[i], 16)
            sp.wait_ge(zero_made, 1)
            for at in range(0, ROWS, CLEAR):
                n = min(CLEAR, ROWS - at) // CLEAR_ROWS
                sp.dma_start(expert_in[at:at + n * CLEAR_ROWS, :].rearrange("(p a) c -> p (a c)", a=CLEAR_ROWS),
                             as_f32(halves[0:n, 0:CLEAR_ROWS * C])).then_inc(cleared, 16)

            def load_rows(r, e, n):
                u = r * E + e
                wait_past(sp, xg_turned, [u * NG, u * NG, u * NG + 1][n])
                buf = n % 2
                s, m = GROUPS[n]
                full = m // P
                at = e * CAP + s
                sp.dma_start(xg[buf][:, 0:full, :],
                             expert_in[bass.ds(at, full * P), :].rearrange(tok, p=P)).then_inc(xg_loaded[buf], 16)
                if m % P:
                    sp.dma_start(xg[buf][0:m % P, full, :],
                                 expert_in[bass.ds(at + full * P, m % P), :]).then_inc(xg_loaded[buf], 16)

            def stage_fc(r, e):
                wait_past(sp, fc_split, (r * E + e) * 8)
                sp.dma_start(raw_fc, w_fc[e].rearrange("(a p) n -> p a n", p=P)).then_inc(fc_staged, 16)
                sp.dma_start(raw_g, w_g[e].rearrange("(a p) n -> p a n", p=P)).then_inc(fc_staged, 16)

            def stage_proj(r, e):
                wait_past(sp, proj_split, (r * E + e) * 4)
                sp.dma_start(raw_proj, w_proj[e].rearrange("(a p) n -> p a n", p=P)).then_inc(proj_staged, 16)

            def load_bias(r, e):
                sp.dma_start(y_bias, b_proj[e].to_broadcast([P, C])).then_inc(bias_loaded, 16)

            def store_y(r, e, t):
                u = r * E + e
                sp.wait_ge(y_copied, u * Y_TILES + t + 1)
                n = t // 4 if t < 8 else 2
                o, m = GROUP_TILES[n][t - 4 * n]
                at = e * CAP + GROUPS[n][0] + o
                sp.dma_start(expert_out[bass.ds(at, m), :], y_sb[0:m, t % 2, :]).then_inc(y_stored[t % 2], 16)

            def stage_attention(n, *producer):
                w = (w_q, w_k, w_gate, w_v, w_o)[n]
                sp.wait_ge(*producer)
                sp.dma_start(raw_w[n].rearrange("p (a n) -> p a n", a=w.shape[0] // P),
                             w.rearrange("(a p) n -> p a n", p=P)).then_inc(aw_staged[n], 16)

            def expert(r, e, last):
                load_rows(r, e, 2)
                if not last:
                    stage_fc(r, e + 1)
                    stage_proj(r, e + 1)
                elif r == 0:
                    stage_attention(0, fc_split, E * 8)
                    stage_attention(1, fc_split, E * 8)
                    stage_attention(2, proj_split, E * 4)
                    stage_attention(3, xg_turned, E * NG)
                for t in range(4):
                    store_y(r, e, t)
                if not last:
                    load_rows(r, e + 1, 0)
                    load_rows(r, e + 1, 1)
                elif r == 0:
                    stage_attention(4, s_split, E * UNITS)
                for t in range(4, Y_TILES):
                    store_y(r, e, t)
                if not last:
                    load_bias(r, e + 1)

            for r in range(2):
                quarter = (r + 1) * TOPK * QT * 16
                sp.wait_ge(scattered[0], quarter)
                sp.wait_ge(scattered[1], quarter)
                stage_fc(r, 0)
                sp.wait_ge(scattered[2], quarter)
                stage_proj(r, 0)
                sp.wait_ge(scattered[3], quarter)
                load_rows(r, 0, 0)
                load_rows(r, 0, 1)
                load_bias(r, 0)
                with sp.Fori(0, E - 1) as e:
                    expert(r, e, False)
                expert(r, E - 1, True)
            with sp.Fori(0, TILES) as i:
                sp.wait_ge(combined, TILES + i + 1)
                sp.dma_start(out[0, bass.ds(i * P, P), :], x[:, bass.ds(i, 1), :].rearrange("p a c -> p (a c)")).then_inc(stored, 16)
            sp.wait_ge(stored, TILES * 16)

        @block.gpsimd
        def _(pool):
            steps = Steps(pool, pool_steps)
            steps.after(nc.gpsimd.memset(ident[:], 0.0))
            steps.after(nc.gpsimd.memset(causal[:], 1.0))
            steps.after(nc.gpsimd.memset(before[:], 1.0))
            nc.gpsimd.affine_select(out=ident[:], in_=ident[:], compare_op=ALU.not_equal, fill=1.0, base=0,
                                    pattern=[[-1, P]], channel_multiplier=1).then_inc(consts_made, 1)
            nc.gpsimd.affine_select(out=causal[:], in_=causal[:], compare_op=ALU.is_ge, fill=0.0, base=0,
                                    pattern=[[1, P]], channel_multiplier=-1).then_inc(consts_made, 1)
            nc.gpsimd.affine_select(out=before[:], in_=before[:], compare_op=ALU.is_gt, fill=0.0, base=0,
                                    pattern=[[1, P]], channel_multiplier=-1).then_inc(consts_made, 1)
            nc.gpsimd.memset(limit[:], LIMIT).then_inc(consts_made, 1)
            nc.gpsimd.iota(rank[:], [[-1, E]], base=E, channel_multiplier=0,
                           allow_small_or_imprecise_dtypes=True).then_inc(consts_made, 1)
            for r in range(2):
                for n, (k, first, tiles) in enumerate(BLOCKS):
                    pool.wait_ge(slots_made, r * len(BLOCKS) + n + 1)
                    if r == 0 and n == 0:
                        pool.wait_ge(cleared, CLEARS * 16)
                    for i in range(first, first + tiles):
                        j = k * TILES + i
                        pool.indirect_dma_start(expert_in,
                                                bass.IndirectOffsetOnAxis(ap=write_slot[:, j:j + 1], axis=0),
                                                xn[:, i, :], None, bounds_check=ROWS - 1,
                                                oob_is_err=False).then_inc(scattered[i // QT], 16)
                def gather(into, k, i, landed):
                    j = k * TILES + i
                    pool.indirect_dma_start(into, None, expert_out,
                                            bass.IndirectOffsetOnAxis(ap=read_slot[:, j:j + 1], axis=0)
                                            ).then_inc(landed, 16)

                def wait_stored(experts):
                    for b in range(2):
                        pool.wait_ge(y_stored[b], (experts * Y_TILES // 2 + 1) * 16)

                if r == 0:
                    wait_stored(E)
                    for i in range(TILES):
                        if i >= SUPER:
                            pool.wait_ge(combined, i - SUPER + 1)
                        for k in range(TOPK):
                            gather(got4[:, i % SUPER, k, :], k, i, rows_got[i % SUPER])
                else:
                    wait_stored(2 * E - 1)
                    for i in range(TILES):
                        if i == 0:
                            pool.wait_ge(fc_split, 2 * E * 8)
                        elif i == 4096 // C:
                            pool.wait_ge(proj_split, 2 * E * 4)
                        elif i == 6144 // C:
                            pool.wait_ge(xg_turned, 2 * E * NG)
                        gather(got[0][:, i, :], 0, i, earlier_got)
                    wait_stored(2 * E)
                    for i in range(TILES):
                        gather(got[1][:, i, :], 1, i, rows_got[i])

        @block.tensor
        def _(pe):
            pe.wait_ge(consts_made, CONSTS)
            pe.wait_ge(small_loaded, 16 * 5)
            for n, (k, at) in enumerate(((E * HJ, 0), (E * HJ, P), (NPAIR, 2 * P))):
                pe.transpose(bank[n][:, 0:k], rows[0:k, at:at + P], ident[0:k, 0:k]).then_inc(bias_turned, 1)

            def route(r):
                def turn_xn(s):
                    pe.wait_ge(xn_made, (r * NSUP + s + 1) * SUPER)
                    for kc in range(KC):
                        for b in range(SUPER):
                            m = pe.transpose(bank[6 * (s % 2) + kc][:, b * P:(b + 1) * P],
                                             xn[:, s * SUPER + b, kc * P:(kc + 1) * P], ident[:])
                    m.then_inc(xn_turned, 1)

                def count(n):
                    k, first, tiles = BLOCKS[n]
                    cols = slice((k * TILES + first) * E, (k * TILES + first + tiles) * E)
                    pe.wait_ge(hot_made[k], r * QUARTERS + (QUARTERS if k else n + 1))
                    if n:
                        pe.wait_ge(slots_made, r * len(BLOCKS) + n)
                    pe.matmul(bank[3][:, cols], before[:], hot[:, cols], start=True, stop=True)
                    pe.matmul(bank[4][:, cols], ones, hot[:, cols], start=True, stop=True).then_inc(counted, 1)

                turn_xn(0)
                for s in range(NSUP):
                    if s + 1 < NSUP:
                        turn_xn(s + 1)
                    pe.wait_ge(xnt_copied, (r * NSUP + s + 1) * KC)
                    for b in range(SUPER):
                        i = s * SUPER + b
                        for kc in range(KC):
                            m = pe.matmul(bank[(2, 5)[i // QT % 2]][:, i * E:(i + 1) * E], xnt[s % 2][:, kc, b * P:(b + 1) * P],
                                          router[:, kc, :], start=(kc == 0), stop=(kc == KC - 1))
                    m.then_inc(logits_done, 1)
                    if s > 1 and s % 2:
                        count(s // 2 - 1)
                count(QUARTERS - 1)
                count(QUARTERS)

            def turn(r, e, n):
                u = r * E + e
                buf = n % 2
                pe.wait_ge(xg_loaded[buf], [u * 48 + 16, u * 16 + 16, u * 48 + 48][n])
                wait_past(pe, xt_split, u * NG + n)
                for kc in range(KC):
                    for i, (o, m) in enumerate(GROUP_TILES[n]):
                        t = pe.transpose(bank[6 + kc][:, o:o + m], xg[buf][0:m, i, kc * P:(kc + 1) * P],
                                         ident[0:m, 0:m])
                t.then_inc(xg_turned, 1)

            def up(r, e, n, js, width=None):
                u = r * E + e
                buf, w = n % 2, width or GROUPS[n][1]
                if js[0] == 0:
                    pe.wait_ge(xt_split, u * NG + n + 1)
                    if n == 0:
                        pe.wait_ge(fc_split, u * 8 + 8)
                for j in js:
                    unit = n * HJ + j
                    b = unit % 2
                    if unit >= 2:
                        pe.wait_ge(hg_made, u * UNITS + unit - 1)
                    for at, hi_lo in ((0, (fc_hi, fc_lo)), (2, (gw_hi, gw_lo))):
                        ps = [(kc, a, v) for kc in range(KC) for a, v in passes(hi_lo, (xt_hi[buf], xt_lo[buf]))]
                        for i, (kc, a, v) in enumerate(ps):
                            m = pe.matmul(bank[at + b][:, 0:w], a[:, kc, j * P:(j + 1) * P], v[:, kc, 0:w],
                                          start=(i == 0), stop=(i == len(ps) - 1))
                    m.then_inc(up_done, 1)

            def down(r, e, n, tiles=range(SUPER)):
                u = r * E + e
                buf = n % 2
                pe.wait_ge(s_split, u * UNITS + (n + 1) * HJ)
                if n == 0:
                    pe.wait_ge(proj_split, u * 4 + 4)
                for i, (o, m) in enumerate(GROUP_TILES[n]):
                    if i not in tiles:
                        continue
                    t = 4 * n + i
                    if t >= 2:
                        pe.wait_ge(y_copied, u * Y_TILES + t - 1)
                    ps = [(j, a, v) for j in range(HJ)
                          for a, v in passes((s_hi[buf], s_lo[buf]), (pr_hi, pr_lo))]
                    for k, (j, a, v) in enumerate(ps):
                        mm = pe.matmul(bank[4 + t % 2][0:m, 0:C], a[:, j, o:o + m], v[:, j, :],
                                       start=(k == 0), stop=(k == len(ps) - 1))
                    mm.then_inc(y_done, 1)

            def expert(r, e, last):
                first, second = range(HJ // 2), range(HJ // 2, HJ)
                up(r, e, 0, first)
                turn(r, e, 1)
                up(r, e, 0, second)
                wide1 = fills_group1(pe, e)

                def up1(js):
                    with pe.If(wide1):
                        up(r, e, 1, js)
                    with pe.Else():
                        up(r, e, 1, js, NARROW)

                up1(first)
                turn(r, e, 2)
                up1(second)
                down(r, e, 0)
                last_group = has_last_group(pe, e)
                with pe.If(last_group):
                    up(r, e, 2, range(HJ))
                with pe.Else():
                    pe.drain().then_inc(up_done, HJ)
                down(r, e, 1, range(2))
                if not last:
                    turn(r, e + 1, 0)
                down(r, e, 1, range(2, 3))
                with pe.If(wide1):
                    down(r, e, 1, range(3, 4))
                with pe.Else():
                    pe.drain().then_inc(y_done, 1)
                with pe.If(last_group):
                    down(r, e, 2)
                with pe.Else():
                    pe.drain().then_inc(y_done, len(GROUP_TILES[2]))

            def attention():
                def turn_x(s):
                    pe.wait_ge(xna_made, s * SUPER + SUPER)
                    for kc in range(KC):
                        for b in range(SUPER):
                            m = pe.transpose(bank[kc][:, b * P:(b + 1) * P], xna[:, b, kc * P:(kc + 1) * P], ident[:])
                    m.then_inc(xna_turned, 1)

                def project(at, w, g):
                    ps = [(kc, a, v) for kc in range(KC) for a, v in passes(w, xa)]
                    for i, (kc, a, v) in enumerate(ps):
                        m = pe.matmul(bank[at][:], a[:, kc, g * P:(g + 1) * P], v[:, kc, :],
                                      start=(i == 0), stop=(i == len(ps) - 1))
                    return m

                def project_z(s, g):
                    project(2, wz, g).then_inc(z_done, 1)

                def project_qk(s, g):
                    project(0, wq, g).then_inc(q_done, 1)
                    project(1, wk, g).then_inc(k_done, 1)

                def values(s):
                    for b in range(SUPER):
                        if b == SUPER // 2:
                            pe.wait_ge(z_used, s * NPAIR + 1)
                            project_z(s, 1)
                        for half in range(2):
                            n = 2 * b + half
                            if n >= 2:
                                pe.wait_ge(v_copied, s * 8 + n - 1)
                            ps = [(kc, a, v) for kc in range(KC) for a, v in passes(xa, wv)]
                            for i, (kc, a, v) in enumerate(ps):
                                m = pe.matmul(bank[5 + n % 2][:], a[:, kc, b * P:(b + 1) * P],
                                              v[:, kc, half * 512:(half + 1) * 512],
                                              start=(i == 0), stop=(i == len(ps) - 1))
                            m.then_inc(v_done, 1)

                def scores(s, g):
                    G = s * NPAIR + g
                    pe.wait_ge(qk_made, G + 1)
                    for c in range(SUPER):
                        m = pe.transpose(bank[6][:, c * P:(c + 1) * P], kd[:, c, :], ident[:])
                    m.then_inc(k_turned, 1)
                    if g:
                        pe.wait_ge(prob_made, G)
                    for c in range(SUPER):
                        for h in range(2):
                            hp = slice(h * DH, (h + 1) * DH)
                            m = pe.matmul(bank[3 + h][:, c * P:(c + 1) * P], kd[hp, c, :], qd[g % 2][hp, c, :],
                                          start=True, stop=True)
                    m.then_inc(scores_done, 1)

                def additions(s, g):
                    G = s * NPAIR + g
                    pe.wait_ge(kdt_copied, G + 1)
                    if g:
                        pe.wait_ge(state_kept, G)
                    kv = bank[7][:, 0:DH * (SUPER + 2)].rearrange("p (n c) -> p n c", n=DH)
                    for c in range(SUPER):
                        for h in range(2):
                            hp = slice(h * DH, (h + 1) * DH)
                            m = pe.matmul(kv[hp, :, c + 2], kdt[:, c, hp], v_sb[:, c, g * P + h * DH:g * P + (h + 1) * DH],
                                          start=True, stop=True)
                    m.then_inc(kv_done, 1)

                def outputs(s, g):
                    G = s * NPAIR + g
                    pe.wait_ge(prob_made, G + 1)
                    if g:
                        pe.wait_ge(ot_split, G)
                    pe.wait_ge(state_ready, G + 1)
                    for c in range(SUPER):
                        cols = slice(c * P, (c + 1) * P)
                        pe.matmul(bank[5][:, cols], state_in[:, c, :], qd[g % 2][:, c, :],
                                  start=True, stop=False, skip_group_check=True)
                        for h in range(2):
                            m = pe.matmul(bank[5][h * DH:(h + 1) * DH, cols],
                                          v_sb[:, c, g * P + h * DH:g * P + (h + 1) * DH], prob[h][:, c, :],
                                          start=False, stop=True, skip_group_check=True)
                    m.then_inc(o_done, 1)

                def out_projection(s):
                    pe.wait_ge(ot_split, s * NPAIR + NPAIR)
                    for b in range(SUPER):
                        if b >= 2:
                            pe.wait_ge(wo_added, s * SUPER + b - 1)
                        ps = [(g, a, v) for g in range(NPAIR) for a, v in passes(ot, wo)]
                        for i, (g, a, v) in enumerate(ps):
                            m = pe.matmul(bank[3 + b % 2][:, 0:C], a[:, g, b * P:(b + 1) * P], v[:, g, :],
                                          start=(i == 0), stop=(i == len(ps) - 1))
                        m.then_inc(wo_done, 1)

                def supertile(s, last):
                    for g in range(NPAIR):
                        G = s * NPAIR + g
                        if g == 0:
                            pe.wait_ge(v_copied, s * 8 + 8)
                        elif g + 1 < NPAIR:
                            pe.wait_ge(z_used, G + 1)
                            project_z(s, g + 1)
                        scores(s, g)
                        if g + 1 == NPAIR and not last:
                            turn_x(s + 1)
                        if g == 0:
                            project_qk(s, 1)
                        else:
                            outputs(s, g - 1)
                        additions(s, g)
                        if 0 < g < NPAIR - 1:
                            project_qk(s, g + 1)
                    if not last:
                        pe.wait_ge(xa_split, (s + 1) * KC + KC)
                        project_z(s + 1, 0)
                        project_qk(s + 1, 0)
                    outputs(s, NPAIR - 1)
                    out_projection(s)
                    if not last:
                        values(s + 1)
                        pe.wait_ge(wo_added, s * SUPER + SUPER)
                        pe.wait_ge(state_kept, s * NPAIR + NPAIR)

                pe.wait_ge(aw_split, 5)
                pe.wait_ge(att_cleared, ATT_CLEARS)
                turn_x(0)
                pe.wait_ge(xa_split, KC)
                project_z(0, 0)
                project_qk(0, 0)
                values(0)
                with pe.Fori(0, NSUP - 1) as s:
                    supertile(s, False)
                supertile(NSUP - 1, True)

            for r in range(2):
                route(r)
                turn(r, 0, 0)
                pe.wait_ge(long_made, 2 * r + 2)
                with pe.Fori(0, E - 1) as e:
                    expert(r, e, False)
                expert(r, E - 1, True)
                if r == 0:
                    attention()

        @block.scalar
        def _(act):
            def copy(o, i):
                return nc.scalar.activation(o, i, ACT.Copy)

            def deviation(n, tiles):
                act.wait_ge(var_made, n)
                nc.scalar.activation(rstd[:, tiles], rstd[:, tiles], ACT.Sqrt).then_inc(std_made, 1)

            def route(r):
                if r:
                    deviation(QUARTERS + 1, slice(0, TILES))
                for s in range(NSUP):
                    if r == 0 and s % 2 == 0:
                        for q in range(0 if s == 0 else s // 2 + 1, min(s // 2 + 2, QUARTERS)):
                            deviation(q + 1, slice(q * QT, q * QT + QT))
                    act.wait_ge(xn_turned, r * NSUP + s + 1)
                    for kc in range(KC):
                        copy(xnt[s % 2][:, kc, :], bank[6 * (s % 2) + kc][:]).then_inc(xnt_copied, 1)
                act.wait_ge(gap_made, (r + 1) * QUARTERS)
                nc.scalar.activation(weight2[:], weight2[:], ACT.Exp).then_inc(exp_made, 1)

            def split_fc(u, k):
                raw, hi = ((raw_fc, fc_hi), (raw_g, gw_hi))[k // 4]
                at = (slice(None), k % 4 // 2, slice(k % 2 * 512, k % 2 * 512 + 512))
                copy(hi[at], raw[at]).then_inc(fc_hi_made, 1)

            def split_attention(n):
                w = (wq, wk, wz, wv, wo)[n]
                act.wait_ge(aw_staged[n], 16)
                copy(w[0].rearrange("p a n -> p (a n)"), raw_w[n]).then_inc(aw_hi_made, 1)

            def turned(r, e, n):
                w, buf = GROUPS[n][1], n % 2
                act.wait_ge(xg_turned, (r * E + e) * NG + n + 1)
                for kc in range(KC):
                    copy(xt_hi[buf][:, kc, 0:w], bank[6 + kc][:, 0:w]).then_inc(xt_hi_made, 1)

            def expert(r, e, last):
                u = r * E + e

                def gate(unit):
                    w, b, j = GROUPS[unit // HJ][1], unit % 2, unit % HJ
                    act.wait_ge(up_done, u * UNITS + unit + 1)
                    nc.scalar.activation(g_sb[b][:, 0:w], bank[2 + b][:, 0:w], ACT.Identity,
                                         bias=bias_now[:, j:j + 1]).then_inc(g_copied, 1)

                def silu(unit):
                    n, j, b = unit // HJ, unit % HJ, unit % 2
                    w = GROUPS[n][1]
                    act.wait_ge(hg_made, u * UNITS + unit + 1)
                    nc.scalar.activation(hg[b][:, 0:w], hg[b][:, 0:w], ACT.Silu).then_inc(silu_made, 1)
                    act.wait_ge(silu_made, u * UNITS + unit + 1)
                    copy(s_hi[n % 2][:, j, 0:w], hg[b][:, 0:w]).then_inc(s_hi_made, 1)

                def units(lo, hi):
                    gate(lo)
                    for unit in range(lo, hi):
                        if unit + 1 < hi:
                            gate(unit + 1)
                        silu(unit)
                        if unit in (HJ // 2, HJ + HJ // 2):
                            turned(r, e, unit // HJ + 1)
                        if 1 <= unit < 5:
                            k = 2 * (unit - 1)
                            act.wait_ge(proj_staged, u * 16 + 16)
                            copy(pr_hi[:, k:k + 2, :], raw_proj[:, k:k + 2, :]).then_inc(proj_hi_made, 1)

                copy(bias_now[:], bias_g[:, bass.ds(e * HJ, HJ)]).then_inc(bias_set, 1)
                act.wait_ge(bias_set, u + 1)
                units(0, 2 * HJ)
                with act.If(has_last_group(act, e)):
                    units(2 * HJ, UNITS)
                with act.Else():
                    act.drain().then_inc(g_copied, HJ)
                    act.drain().then_inc(silu_made, HJ)
                    act.drain().then_inc(s_hi_made, HJ)
                act.wait_ge(g_copied, (u + 1) * UNITS)
                act.sem_inc(biases_used, 1)
                if not last:
                    act.wait_ge(fc_staged, u * 32 + 64)
                    for k in range(8):
                        split_fc(u + 1, k)
                    turned(r, e + 1, 0)
                elif r == 0:
                    split_attention(0)
                    split_attention(1)

            def attention():
                act.wait_ge(y_done, E * Y_TILES)
                for n in range(2, 5):
                    split_attention(n)

                def log_variance(s):
                    act.wait_ge(var4_made, s + 1)
                    nc.scalar.activation(rstd_now, var_now, ACT.Ln).then_inc(log_var4_made, 1)

                def inverse_deviation(s):
                    act.wait_ge(log_var4_made, s + 1)
                    nc.scalar.activation(rstd_now, rstd_now, ACT.Exp, scale=-0.5).then_inc(rstd4_made, 1)

                def split_x(s):
                    act.wait_ge(xna_turned, s + 1)
                    for kc in range(KC):
                        copy(xa[0][:, kc, :], bank[kc][:]).then_inc(xa_hi_made, 1)

                def log_decay(s, g, first=False):
                    G = s * NPAIR + g
                    act.wait_ge(z_done, G + 1)
                    if not first:
                        act.wait_ge(qk_made, G)
                    gate = far[:, :, :, 0:HALF]
                    z = bank[2][:].rearrange("p (a h n) -> p a h n", h=2, n=HALF)
                    nc.scalar.activation(gate, z, ACT.Exp, scale=-1.0, bias=bias_gate[:, g:g + 1]).then_inc(z_used, 1)
                    act.wait_ge(z_used, G + 1)
                    nc.scalar.activation(gate, gate, ACT.Ln, bias=1.0).then_inc(log_made, 1)

                def decays(s, g):
                    G = s * NPAIR + g
                    act.wait_ge(log_summed, G + 1)
                    n, f = near[:, :, :, 0:HALF], far[:, :, :, 0:HALF]
                    nc.scalar.activation(n, f, ACT.Exp, scale=-1.0).then_inc(near_made, 1)
                    act.wait_ge(near_made, G + 1)
                    nc.scalar.activation(f, f, ACT.Exp).then_inc(far_made, 1)

                def turned_keys(s, g):
                    act.wait_ge(k_turned, s * NPAIR + g + 1)
                    copy(kdt.rearrange("p a n -> p (a n)"), bank[6][:]).then_inc(kdt_copied, 1)

                def split_o(s, g):
                    act.wait_ge(o_done, s * NPAIR + g + 1)
                    copy(ot[0][:, g, :], bank[5][:]).then_inc(ot_hi_made, 1)

                def values(s):
                    for n in range(2 * SUPER):
                        act.wait_ge(v_done, s * 8 + n + 1)
                        copy(v_sb[:, n // 2, n % 2 * 512:n % 2 * 512 + 512], bank[5 + n % 2][:]).then_inc(v_copied, 1)
                        if n == SUPER:
                            log_decay(s, 1)

                def supertile(s, last):
                    for g in range(NPAIR):
                        if 0 < g < NPAIR - 1:
                            log_decay(s, g + 1)
                        if g == SUPER + 1 and not last:
                            log_variance(s + 1)
                        turned_keys(s, g)
                        if g + 1 < NPAIR:
                            decays(s, g + 1)
                        elif not last:
                            split_x(s + 1)
                        if g:
                            split_o(s, g - 1)
                        if g == SUPER + 1 and not last:
                            inverse_deviation(s + 1)
                    if not last:
                        log_decay(s + 1, 0)
                    split_o(s, NPAIR - 1)
                    if not last:
                        decays(s + 1, 0)
                        values(s + 1)

                log_variance(0)
                inverse_deviation(0)
                split_x(0)
                log_decay(0, 0, first=True)
                decays(0, 0)
                values(0)
                with act.Fori(0, NSUP - 1) as s:
                    supertile(s, False)
                supertile(NSUP - 1, True)

            for r in range(2):
                route(r)
                act.wait_ge(fc_staged, r * E * 32 + 32)
                for k in range(8):
                    split_fc(r * E, k)
                turned(r, 0, 0)
                act.wait_ge(long_made, 2 * r + 2)
                with act.Fori(0, E - 1) as e:
                    expert(r, e, False)
                expert(r, E - 1, True)
                if r == 0:
                    attention()

        @block.vector
        def _(dve):
            steps = Steps(dve, dve_steps)
            v = nc.vector

            v.memset(as_f32(halves[:, 0:CLEAR_ROWS * C]), 0.0).then_inc(zero_made, 1)
            dve.wait_ge(small_loaded, 16 * 5)
            dve.wait_ge(consts_made, CONSTS)
            for n, o in enumerate((bias_fc, bias_g, bias_gate)):
                dve.wait_ge(bias_turned, n + 1)
                steps.after(v.tensor_scalar(o[:], bank[n][:, 0:o.shape[1]], -1.0 if o is bias_gate else 1.0, None,
                                            ALU.mult))

            def tile_of(t, i):
                return t[:, bass.ds(i, 1), :].rearrange("p a c -> p (a c)")

            def tile_stats(i):
                return v.bn_stats(tile_of(stats, i), tile_of(x, i))

            def variance(halves_of, mean, var, out_):
                mean1, sq1, mean2, sq2 = (halves_of[:, :, n] for n in (1, 2, 4, 5))
                steps.after(v.tensor_tensor(out_, mean1, mean2, ALU.subtract))
                steps.after(v.tensor_tensor(out_, out_, out_, ALU.mult))
                steps.after(v.tensor_tensor(var, sq1, sq2, ALU.add))
                steps.after(v.tensor_scalar(var, var, 1.0 / C, EPS, ALU.mult, ALU.add))
                steps.after(v.tensor_tensor(mean, mean1, mean2, ALU.add))
                steps.after(v.tensor_scalar(mean, mean, 0.5, None, ALU.mult))
                return v.scalar_tensor_tensor(out_, out_, 0.25, var, ALU.mult, ALU.add)

            def inverse_deviation(n, tiles):
                of = stats[:, tiles, :]
                variance(of, of[:, :, 1], of[:, :, 2], rstd[:, tiles]).then_inc(var_made, 1)
                dve.wait_ge(std_made, n)
                steps.after(v.reciprocal(rstd[:, tiles], rstd[:, tiles]))

            def choose(of, k, q):
                tiles = slice(q * QT, q * QT + QT)
                wide_ = [P, QT, E]
                ranks = rank[:].unsqueeze(1).to_broadcast(wide_)
                t, found = top[k], best[:, k * TILES + q * QT:k * TILES + q * QT + QT]
                steps.after(v.tensor_reduce(t, of, AX_X, ALU.max))
                steps.after(v.tensor_tensor(chosen, of, t.unsqueeze(2).to_broadcast(wide_), ALU.is_equal))
                steps.after(v.tensor_tensor(chosen, chosen, ranks, ALU.mult))
                steps.after(v.tensor_reduce(found, chosen, AX_X, ALU.max))
                steps.after(v.tensor_tensor(chosen, ranks, found.unsqueeze(2).to_broadcast(wide_), ALU.is_equal))
                if k == 0:
                    picks = hot[:, q * QT * E:(q + 1) * QT * E].rearrange("p (e j) -> p j e", e=E)
                else:
                    picks = hot[:, TILES * E:PICKS * E].rearrange("p (e j) -> p j e", e=E)[:, tiles, :]
                v.tensor_copy(picks, chosen).then_inc(hot_made[k], 1)

            def choices(r, q):
                tiles = slice(q * QT, q * QT + QT)
                of = logits
                dve.wait_ge(logits_done, r * NSUP + 2 * q + 2)
                steps.after(v.tensor_tensor(of, bank[(2, 5)[q % 2]][:, q * QT * E:(q + 1) * QT * E].rearrange("p (i e) -> p i e", e=E),
                                            router_bias[:].unsqueeze(1).to_broadcast([P, QT, E]), ALU.add))
                choose(of, 0, q)
                dve.wait_ge(hot_made[0], r * QUARTERS + q + 1)
                steps.after(v.scalar_tensor_tensor(of, chosen, -BIG, of, ALU.mult, ALU.add))
                choose(of, 1, q)
                v.tensor_tensor(weight2[:, tiles], top[1], top[0], ALU.subtract).then_inc(gap_made, 1)
                dve.wait_ge(gap_made, r * QUARTERS + q + 1)

            def set_resume(tiles):
                t = resume[:, 0:tiles * E]
                steps.after(v.memset(t, 1.0))
                steps.after(v.memset(t.rearrange("p (e j) -> p e j", e=E)[:, :, 0:1], 0.0))

            def give_slots(r, n):
                k, first, tiles = BLOCKS[n]
                picks = slice(k * TILES + first, k * TILES + first + tiles)
                cols = slice(picks.start * E, picks.stop * E)
                t = taken[:, 0:tiles * E]
                by_expert = t.rearrange("p (e j) -> p e j", e=E)
                psum = [bank[i][:, cols].rearrange("p (e j) -> p e j", e=E) for i in (3, 4)]
                ov, fs, at = over[:, 0:tiles], first_slot[:, 0:tiles], pos[:, picks]
                dve.wait_ge(counted, r * len(BLOCKS) + n + 1)
                steps.after(v.tensor_tensor_scan(t, resume[:, 0:tiles * E], bank[4][:, cols], 0.0, ALU.mult, ALU.add))
                earlier, now = given[n % 2], given[(n + 1) % 2]
                steps.after(v.tensor_tensor(now, earlier, by_expert[:, :, tiles - 1], ALU.add))
                steps.after(v.tensor_tensor(by_expert, by_expert, psum[1], ALU.subtract))
                steps.after(v.tensor_tensor(by_expert, by_expert, psum[0], ALU.add))
                steps.after(v.tensor_tensor(by_expert, by_expert, earlier.unsqueeze(2).to_broadcast([P, E, tiles]),
                                            ALU.add))
                steps.after(v.tensor_tensor(t, t, hot[:, cols], ALU.mult))
                steps.after(v.tensor_reduce(at, t.rearrange("p (e j) -> p j e", e=E), AX_X, ALU.add))
                steps.after(v.tensor_scalar(fs, best[:, picks], -float(CAP), float(E * CAP), ALU.mult, ALU.add))
                steps.after(v.tensor_scalar(ov, at, float(CAP), float(SKIP), ALU.is_ge, ALU.mult))
                steps.after(v.tensor_tensor(ov, ov, fs, ALU.add))
                v.tensor_tensor(write_slot[:, picks], ov, at, ALU.add).then_inc(slots_made, 1)
                dve.wait_ge(slots_made, r * len(BLOCKS) + n + 1)
                steps.after(v.tensor_scalar(ov, at, float(CAP - 1), None, ALU.min))
                steps.after(v.tensor_tensor(reads[k][:, first:first + tiles], ov, fs, ALU.add))

            def route(r):
                def rows_of(q):
                    if r == 0:
                        dve.wait_ge(x_loaded[q], 16)
                        for t in range(q * QT, (q + 1) * QT):
                            v.bn_stats(stats[:, t, :], x[:, t, :]).then_inc(stats_made, 1)
                        dve.wait_ge(stats_made, (q + 1) * QT)
                        inverse_deviation(q + 1, slice(q * QT, (q + 1) * QT))
                    elif q == 0:
                        dve.wait_ge(stats_made, 2 * TILES)
                        inverse_deviation(QUARTERS + 1, slice(0, TILES))
                    for i in range(q * QT, (q + 1) * QT):
                        v.tensor_scalar(xn[:, i, :], x[:, i, :], stats[:, i, 1:2], rstd[:, i:i + 1],
                                        ALU.subtract, ALU.mult).then_inc(xn_made, 1)

                rows_of(0)
                steps.after(v.memset(ones, 1.0))
                steps.after(v.memset(given[0], 0.0))
                set_resume(QT)
                rows_of(1)
                for q in range(QUARTERS):
                    if q + 2 < QUARTERS:
                        rows_of(q + 2)
                    choices(r, q)
                    give_slots(r, q)
                set_resume(TILES)
                give_slots(r, QUARTERS)
                for n, rows_ in enumerate((GROUPS[2][0], GROUPS[1][0] + NARROW)):
                    v.tensor_scalar(long[:, n * E:(n + 1) * E], given[(QUARTERS + 1) % 2][0:1, :], float(rows_), None,
                                    ALU.is_gt).then_inc(long_made, 1)
                dve.wait_ge(long_made, 2 * r + 2)
                steps.after(v.tensor_tensor(over, reads[0], reads[1], ALU.is_lt))
                steps.after(v.tensor_tensor(read_slot[:, 0:TILES], reads[0], reads[1], ALU.min))
                steps.after(v.tensor_tensor(read_slot[:, TILES:PICKS], reads[0], reads[1], ALU.max))
                dve.wait_ge(exp_made, r + 1)
                steps.after(v.tensor_scalar(weight1[:], weight2[:], 1.0, None, ALU.add))
                steps.after(v.reciprocal(weight1[:], weight1[:]))
                steps.after(v.scalar_tensor_tensor(weight2[:], weight2[:], 0.5, weight1[:], ALU.mult, ALU.mult))
                steps.after(v.tensor_scalar(weight1[:], weight1[:], 0.5, None, ALU.mult))
                kept = [first_slot, reads[1]]
                for k, w in enumerate((weight1, weight2)):
                    steps.after(v.tensor_tensor(kept[k], w[:], over, ALU.mult))
                    steps.after(v.tensor_tensor(w[:], w[:], kept[k], ALU.subtract))
                steps.after(v.tensor_tensor(kept[0], kept[0], weight2[:], ALU.add))
                steps.after(v.tensor_tensor(weight2[:], kept[1], weight1[:], ALU.add))
                steps.after(v.tensor_copy(weight1[:], kept[0]))

            def split_fc(done, k):
                raw, hi, lo = ((raw_fc, fc_hi, fc_lo), (raw_g, gw_hi, gw_lo))[k // 4]
                at = (slice(None), k % 4 // 2, slice(k % 2 * 512, k % 2 * 512 + 512))
                dve.wait_ge(fc_hi_made, done + k + 1)
                v.tensor_tensor(lo[at], raw[at], as_f32(hi[at]), ALU.subtract).then_inc(fc_split, 1)

            def split_attention(n):
                w = (wq, wk, wz, wv, wo)[n]
                dve.wait_ge(aw_hi_made, n + 1)
                v.tensor_tensor(w[1].rearrange("p a n -> p (a n)"), raw_w[n],
                                as_f32(w[0].rearrange("p a n -> p (a n)")), ALU.subtract).then_inc(aw_split, 1)

            def turned(r, e, n):
                w, buf = GROUPS[n][1], n % 2
                for kc in range(KC):
                    dve.wait_ge(xt_hi_made, ((r * E + e) * NG + n) * KC + kc + 1)
                    i = v.tensor_tensor(xt_lo[buf][:, kc, 0:w], bank[6 + kc][:, 0:w],
                                        as_f32(xt_hi[buf][:, kc, 0:w]), ALU.subtract)
                i.then_inc(xt_split, 1)

            def expert(r, e, last):
                u = r * E + e

                def product(unit):
                    w, b, col = GROUPS[unit // HJ][1], unit % 2, e * HJ + unit % HJ
                    dve.wait_ge(g_copied, u * UNITS + unit + 1)
                    if unit >= 2:
                        dve.wait_ge(s_split, u * UNITS + unit - 1)
                    v.scalar_tensor_tensor(hg[b][:, 0:w], bank[b][:, 0:w], bias_fc[:, bass.ds(col, 1)],
                                           g_sb[b][:, 0:w], ALU.add, ALU.mult).then_inc(hg_made, 1)

                def low(unit):
                    n, j, b = unit // HJ, unit % HJ, unit % 2
                    w, buf = GROUPS[n][1], n % 2
                    dve.wait_ge(s_hi_made, u * UNITS + unit + 1)
                    v.tensor_tensor(s_lo[buf][:, j, 0:w], hg[b][:, 0:w], as_f32(s_hi[buf][:, j, 0:w]),
                                    ALU.subtract).then_inc(s_split, 1)

                def project_low(k):
                    dve.wait_ge(proj_hi_made, u * 4 + k + 1)
                    at = (slice(None), slice(2 * k, 2 * k + 2), slice(None))
                    v.tensor_tensor(pr_lo[at], raw_proj[at], as_f32(pr_hi[at]), ALU.subtract).then_inc(proj_split, 1)

                def y_out(t):
                    n = t // 4 if t < 8 else 2
                    m = GROUP_TILES[n][t - 4 * n][1]
                    dve.wait_ge(y_done, u * Y_TILES + t + 1)
                    dve.wait_ge(y_stored[t % 2], (u * (Y_TILES // 2) + t // 2 + 1) * 16)
                    v.tensor_tensor(y_sb[0:m, t % 2, :], bank[4 + t % 2][0:m, 0:C], y_bias[0:m, :],
                                    ALU.add).then_inc(y_copied, 1)

                for unit in range(2 * HJ):
                    product(unit)
                    if unit:
                        low(unit - 1)
                    if unit in (HJ // 2 + 1, HJ + HJ // 2 + 1):
                        turned(r, e, unit // HJ + 1)
                    if 2 <= unit < 6:
                        project_low(unit - 2)
                low(2 * HJ - 1)
                dve.wait_ge(bias_loaded, u * 16 + 16)
                for t in range(4):
                    y_out(t)
                with dve.If(has_last_group(dve, e)):
                    for unit in range(2 * HJ, UNITS):
                        product(unit)
                        if unit > 2 * HJ:
                            low(unit - 1)
                    low(UNITS - 1)
                with dve.Else():
                    dve.drain().then_inc(hg_made, HJ)
                    dve.drain().then_inc(s_split, HJ)
                dve.wait_ge(s_split, (u + 1) * UNITS)
                for t in range(4, Y_TILES):
                    if not last and t < 8:
                        split_fc(u * 8 + 8, 2 * (t - 4))
                        split_fc(u * 8 + 8, 2 * (t - 4) + 1)
                    if not last and t == 7:
                        turned(r, e + 1, 0)
                    if last and r == 0 and t in (6, 8):
                        split_attention((t - 6) // 2)
                    y_out(t)

            def add_rows(r, i, got_rows):
                for k, w in enumerate((weight1, weight2)):
                    ins = v.scalar_tensor_tensor(tile_of(x, i), got_rows[:, k, :], w[:, bass.ds(i, 1)],
                                                 tile_of(x, i), ALU.mult, ALU.add)
                    if k == 0:
                        ins.then_inc(row1_added, 1)
                        dve.wait_ge(row1_added, r * TILES + i + 1)
                    else:
                        ins.then_inc(combined, 1)

            def combine_last():
                dve.wait_ge(earlier_got, TILES * 16)
                for i in range(TILES):
                    v.scalar_tensor_tensor(x[:, i, :], got[0][:, i, :], weight1[:, i:i + 1], x[:, i, :],
                                           ALU.mult, ALU.add).then_inc(row1_added, 1)
                for i in range(TILES):
                    dve.wait_ge(rows_got[i], (TILES // SUPER * TOPK + 1 if i < SUPER else 1) * 16)
                    dve.wait_ge(row1_added, TILES + i + 1)
                    v.scalar_tensor_tensor(x[:, i, :], got[1][:, i, :], weight2[:, i:i + 1], x[:, i, :],
                                           ALU.mult, ALU.add).then_inc(combined, 1)

            def attention():
                for n in range(2, 5):
                    split_attention(n)
                dve.wait_ge(aw_split, 5)
                v.memset(state, 0.0).then_inc(att_cleared, 1)
                v.memset(state_in, 0.0).then_inc(att_cleared, 1)
                v.memset(carry[:, :, 0:1], 0.0).then_inc(att_cleared, 1)
                v.memset(bank[7][:, 0:DH * (SUPER + 2)], 0.0).then_inc(att_cleared, 1)
                for t in (near, far):
                    v.memset(t[:, :, 0, HALF:HALF + 1], 1.0).then_inc(att_cleared, 1)
                for h in range(2):
                    v.memset(prob[h][HALF:P, :, 0:HALF], 0.0).then_inc(att_cleared, 1)
                dve.wait_ge(att_cleared, ATT_CLEARS)
                lower, upper = slice(0, HALF), slice(HALF, P)

                def combine(s, b):
                    dve.wait_ge(rows_got[b], (s + 1) * TOPK * 16)
                    add_rows(0, s * SUPER + b, got4[:, b, :, :])

                def statistics(s, b):
                    i = s * SUPER + b
                    dve.wait_ge(combined, i + 1)
                    dve.sem_inc(x_settled, 1)
                    v.bn_stats(stats_now[:, b, :], tile_of(x, i)).then_inc(stats4_made, 1)

                def variances(s):
                    dve.wait_ge(stats4_made, s * SUPER + SUPER)
                    variance(stats_now, mean_now, step_now, var_now).then_inc(var4_made, 1)

                def refine_deviation(s):
                    dve.wait_ge(rstd4_made, s + 1)
                    steps.after(v.tensor_tensor(step_now, rstd_now, rstd_now, ALU.mult))
                    steps.after(v.tensor_tensor(step_now, step_now, var_now, ALU.mult))
                    steps.after(v.tensor_scalar(step_now, step_now, -0.5, 1.5, ALU.mult, ALU.add))
                    steps.after(v.tensor_tensor(rstd_now, rstd_now, step_now, ALU.mult))

                def normalise(s):
                    for b in range(SUPER):
                        v.tensor_scalar(xna[:, b, :], tile_of(x, s * SUPER + b), mean_now[:, b:b + 1],
                                        rstd_now[:, b:b + 1], ALU.subtract, ALU.mult).then_inc(xna_made, 1)

                def split_x(s):
                    for kc in range(KC):
                        dve.wait_ge(xa_hi_made, s * KC + kc + 1)
                        v.tensor_tensor(xa[1][:, kc, :], bank[kc][:], as_f32(xa[0][:, kc, :]),
                                        ALU.subtract).then_inc(xa_split, 1)

                def sum_logs(s, g):
                    dve.wait_ge(log_made, s * NPAIR + g + 1)
                    for c in range(SUPER):
                        for gates in (far[:, c, 0, HALF - 1::-1], far[:, c, 1, 0:HALF]):
                            ins = v.tensor_tensor_scan(gates, gates, limit[:], 0.0, ALU.add, ALU.min)
                    ins.then_inc(log_summed, 1)

                def scaled(s, g):
                    G = s * NPAIR + g
                    dve.wait_ge(far_made, G + 1)
                    v.tensor_copy(carry[:, g % 2, 1:2], near[:, 0, 0, 0:1])
                    v.tensor_tensor(carry[:, g % 2, 2:SUPER + 1], near[:, 1:SUPER, 0, 0], near[:, 0:SUPER - 1, 1, HALF - 1],
                                    ALU.mult)
                    v.tensor_copy(carry[:, g % 2, SUPER + 1:SUPER + 2], near[:, SUPER - 1, 1, HALF - 1:HALF])
                    bq, bk = (bank[n][:].rearrange("p (a n) -> p a n", n=P) for n in (0, 1))
                    first, second = (slice(None), slice(None), 0, slice(1, HALF + 1)), (slice(None), slice(None), 1, lower)
                    q = qd[g % 2]
                    for o, i, w, part_, at in ((q, bq, far, lower, first), (q, bq, near, upper, second),
                                               (kd, bk, near, lower, first), (kd, bk, far, upper, second)):
                        dve.wait_ge(q_done if o is q else k_done, G + 1)
                        ins = v.tensor_tensor(o[:, :, part_], i[:, :, part_], w[at], ALU.mult)
                    ins.then_inc(qk_made, 1)

                def mask(s, g):
                    G = s * NPAIR + g
                    dve.wait_ge(scores_done, G + 1)
                    if g:
                        dve.wait_ge(o_done, G)
                    for h in range(2):
                        sc = bank[3 + h][:].rearrange("p (a n) -> p a n", n=P)
                        v.tensor_tensor(prob[h][lower, :, :], sc[lower, :, :],
                                        causal[lower, :].unsqueeze(1).to_broadcast([HALF, SUPER, P]), ALU.mult)
                        ins = v.tensor_tensor(prob[h][upper, :, upper], sc[upper, :, upper],
                                              causal[upper, upper].unsqueeze(1).to_broadcast([HALF, SUPER, HALF]),
                                              ALU.mult)
                    ins.then_inc(prob_made, 1)

                def chain(s, g):
                    G = s * NPAIR + g
                    by_value = "p (n c) -> p n c"
                    f, kv, st = (t.rearrange(by_value, n=DH) for t in (factors, bank[7][:, 0:DH * (SUPER + 2)], states))
                    dve.wait_ge(qk_made, G + 1)
                    steps.after(v.tensor_copy(f, carry[:, g % 2, :].unsqueeze(1).to_broadcast([P, DH, SUPER + 2])))
                    dve.wait_ge(kv_done, G + 1)
                    steps.after(v.tensor_copy(kv[:, :, 1], state[:, g, :]))
                    steps.after(v.tensor_tensor_scan(states, bank[7][:, 0:DH * (SUPER + 2)], factors, 0.0,
                                                     ALU.add, ALU.mult))
                    for h in range(2):
                        hp = slice(h * DH, (h + 1) * DH)
                        ins = v.tensor_copy(state_in[hp, :, hp].rearrange("p c n -> p n c"), st[hp, :, 1:SUPER + 1])
                    ins.then_inc(state_ready, 1)
                    v.tensor_copy(state[:, g, :], st[:, :, SUPER + 1]).then_inc(state_kept, 1)
                    dve.wait_ge(state_kept, G + 1)

                def split_o(s, g):
                    dve.wait_ge(ot_hi_made, s * NPAIR + g + 1)
                    v.tensor_tensor(ot[1][:, g, :], bank[5][:], as_f32(ot[0][:, g, :]),
                                    ALU.subtract).then_inc(ot_split, 1)

                def add_output(s, b):
                    i = s * SUPER + b
                    dve.wait_ge(wo_done, i + 1)
                    v.tensor_tensor(tile_of(x, i), bank[3 + b % 2][:, 0:C], tile_of(x, i),
                                    ALU.add).then_inc(wo_added, 1)

                def supertile(s, last):
                    for g in range(NPAIR):
                        if g:
                            chain(s, g - 1)
                        if g + 1 < NPAIR:
                            sum_logs(s, g + 1)
                        elif not last:
                            split_x(s + 1)
                        if not last:
                            if 0 < g <= SUPER:
                                statistics(s + 1, g - 1)
                            if g < SUPER:
                                combine(s + 1, g)
                            elif g == SUPER:
                                variances(s + 1)
                            elif g == SUPER + 2:
                                normalise(s + 1)
                        mask(s, g)
                        if g + 1 < NPAIR:
                            scaled(s, g + 1)
                            if g:
                                split_o(s, g - 1)
                        if g == SUPER + 1 and not last:
                            refine_deviation(s + 1)
                    chain(s, NPAIR - 1)
                    split_o(s, NPAIR - 2)
                    if not last:
                        sum_logs(s + 1, 0)
                    split_o(s, NPAIR - 1)
                    if not last:
                        scaled(s + 1, 0)
                    for b in range(SUPER):
                        add_output(s, b)
                    for b in range(SUPER):
                        i = s * SUPER + b
                        dve.wait_ge(wo_added, i + 1)
                        dve.sem_inc(x_settled, 1)
                        tile_stats(i).then_inc(stats_made, 1)

                for b in range(SUPER):
                    combine(0, b)
                for b in range(SUPER):
                    statistics(0, b)
                variances(0)
                refine_deviation(0)
                normalise(0)
                split_x(0)
                sum_logs(0, 0)
                scaled(0, 0)
                steps.loop(0, NSUP - 1, NPAIR * 3 + 10, lambda s: supertile(s, False))
                supertile(NSUP - 1, True)

            for r in range(2):
                route(r)
                for k in range(8):
                    split_fc(r * E * 8, k)
                turned(r, 0, 0)
                with dve.Fori(0, E - 1) as e:
                    expert(r, e, False)
                expert(r, E - 1, True)
                if r == 0:
                    attention()
            combine_last()


_INS = ["L0_attn_x", "L0_attn_W_q", "L0_attn_W_k", "L0_attn_W_v", "L0_attn_W_gate", "L0_attn_b_gate",
        "L0_attn_W_o", "L0_ffn_router_w", "L0_ffn_router_b", "L0_ffn_w_c_fc", "L0_ffn_b_c_fc",
        "L0_ffn_w_gate", "L0_ffn_b_gate", "L0_ffn_w_c_proj", "L0_ffn_b_c_proj"]


def kernel(**inputs):
    import numpy as _np
    import concourse.bacc as _bacc
    from concourse.bass_utils import run_bass_kernel_spmd as _run

    nc = _bacc.Bacc("TRN2", target_bir_lowering=False, num_devices=1)
    arrays, args = {}, []
    for name in _INS:
        a = _np.ascontiguousarray(inputs[name])
        arrays[f"in_{name}"] = a
        args.append(nc.dram_tensor(f"in_{name}", a.shape, mybir.dt.from_np(a.dtype), kind="ExternalInput").ap())
    args.append(nc.dram_tensor("out_x", (1, T, C), F32, kind="ExternalOutput").ap())
    macaron(nc, *args)
    r = _run(nc, [arrays], core_ids=[0])
    return r.results[0]["out_x"]
```
